# Optimizing a Trainium2 kernel written in Bass

```python
import numpy as np
import jax
import jax.numpy as jnp

def _softmax(x, axis=-1):
    return jax.nn.softmax(x, axis=axis)

def _gelu(x):
    return jax.nn.gelu(x, approximate=True)

def _silu(x):
    return jax.nn.silu(x)

def _sigmoid(x):
    return jax.nn.sigmoid(x)

def _layernorm(x, axis=-1, eps=1e-05):
    m = jnp.mean(x, axis=axis, keepdims=True)
    v = jnp.var(x, axis=axis, keepdims=True)
    return (x - m) / jnp.sqrt(v + eps)

def _scatter_add(tgt, idx, src, axis=0):
    return tgt.at[idx].add(src)

def _segment_sum(src, seg, n):
    return jax.ops.segment_sum(src, seg, n)
kernel_name = 'mk_sandwich_d1_jaxref_r4_d1c13b'

def setup_inputs(seed: int=0):
    np.random.seed(seed)
    _w = jnp.asarray

    def _L0_attn_setup():
        import jax, jax.numpy as jnp
        import numpy as np
        EMBED_DIM = 512
        NUM_HEADS = 16
        HEAD_DIM = EMBED_DIM // NUM_HEADS
        WINDOW = 128
        THETA = 10000.0

        def _rope_cos_sin(seq_len, dim, dtype):
            inv_freq = 1.0 / THETA ** (jnp.arange(0, dim, 2, dtype=jnp.float32) / dim)
            t = jnp.arange(seq_len, dtype=jnp.float32)
            angles = t[:, None] * inv_freq[None, :]
            angles = jnp.repeat(angles, 2, axis=-1)
            return (jnp.cos(angles).astype(dtype), jnp.sin(angles).astype(dtype))

        def _rotate_half(x):
            x2 = x.reshape(*x.shape[:-1], x.shape[-1] // 2, 2)
            rot = jnp.stack([-x2[..., 1], x2[..., 0]], axis=-1)
            return rot.reshape(x.shape)
        key = jax.random.key(seed)
        k1, k2, k3, k4 = jax.random.split(key, 4)
        x = jax.random.normal(k1, (2, 512, EMBED_DIM), dtype=jnp.float32)
        scale = 1.0 / np.sqrt(EMBED_DIM)
        W_qkv = jax.random.normal(k2, (EMBED_DIM, 3 * EMBED_DIM), dtype=jnp.float32) * scale
        W_out = jax.random.normal(k3, (EMBED_DIM, EMBED_DIM), dtype=jnp.float32) * scale
        b_out = jax.random.normal(k4, (EMBED_DIM,), dtype=jnp.float32) * 0.01
        return {'x': x, 'W_qkv': W_qkv, 'W_out': W_out, 'b_out': b_out}
    _L0_attn_in = _L0_attn_setup()

    def _L0_ffn_setup():
        import jax, jax.numpy as jnp
        import numpy as np
        D_MODEL = 512
        D_EXPERT = 2048
        EPS = 1e-08

        def ternary_quant(w):
            scale = jnp.mean(jnp.abs(w)) + EPS
            q = jnp.clip(jnp.round(w / scale), -1.0, 1.0) * scale
            return w + jax.lax.stop_gradient(q - w)
        key = jax.random.key(seed)
        k_x, k_up, k_gate, k_down = jax.random.split(key, 4)
        std_in = 1.0 / np.sqrt(D_MODEL)
        std_exp = 1.0 / np.sqrt(D_EXPERT)
        return {'x': jax.random.normal(k_x, (4, 512, D_MODEL), dtype=jnp.float32), 'W_up': jax.random.normal(k_up, (D_EXPERT, D_MODEL), dtype=jnp.float32) * std_in, 'W_gate': jax.random.normal(k_gate, (D_EXPERT, D_MODEL), dtype=jnp.float32) * std_in, 'W_down': jax.random.normal(k_down, (D_MODEL, D_EXPERT), dtype=jnp.float32) * std_exp}
    _L0_ffn_in = _L0_ffn_setup()
    _d = {'L0_attn_x': _L0_attn_in['x'], 'L0_attn_W_qkv': _L0_attn_in['W_qkv'], 'L0_attn_W_out': _L0_attn_in['W_out'], 'L0_attn_b_out': _L0_attn_in['b_out'], 'L0_ffn_W_up': _L0_ffn_in['W_up'], 'L0_ffn_W_gate': _L0_ffn_in['W_gate'], 'L0_ffn_W_down': _L0_ffn_in['W_down']}
    _x0 = _d['L0_attn_x']
    _d['L0_attn_x'] = jax.random.normal(jax.random.fold_in(jax.random.key(seed), 1), (2, 2048, 512), dtype=_x0.dtype)
    del _x0
    return _d

def reference(L0_attn_x, L0_attn_W_qkv, L0_attn_W_out, L0_attn_b_out, L0_ffn_W_up, L0_ffn_W_gate, L0_ffn_W_down):

    def _L0_attn_ref(x, W_qkv, W_out, b_out):
        import jax, jax.numpy as jnp
        import numpy as np
        EMBED_DIM = 512
        NUM_HEADS = 16
        HEAD_DIM = EMBED_DIM // NUM_HEADS
        WINDOW = 128
        THETA = 10000.0

        def _rope_cos_sin(seq_len, dim, dtype):
            inv_freq = 1.0 / THETA ** (jnp.arange(0, dim, 2, dtype=jnp.float32) / dim)
            t = jnp.arange(seq_len, dtype=jnp.float32)
            angles = t[:, None] * inv_freq[None, :]
            angles = jnp.repeat(angles, 2, axis=-1)
            return (jnp.cos(angles).astype(dtype), jnp.sin(angles).astype(dtype))

        def _rotate_half(x):
            x2 = x.reshape(*x.shape[:-1], x.shape[-1] // 2, 2)
            rot = jnp.stack([-x2[..., 1], x2[..., 0]], axis=-1)
            return rot.reshape(x.shape)
        b, l, e = x.shape
        qkv = jnp.einsum('ble,ef->blf', x, W_qkv)
        qkv = qkv.reshape(b, l, NUM_HEADS, HEAD_DIM, 3)
        qkv = jnp.moveaxis(qkv, (4, 2), (0, 2))
        q, k, v = (qkv[0], qkv[1], qkv[2])
        cos, sin = _rope_cos_sin(l, HEAD_DIM, x.dtype)
        q = q * cos + _rotate_half(q) * sin
        k = k * cos + _rotate_half(k) * sin
        i = jnp.arange(l)[:, None]
        j = jnp.arange(l)[None, :]
        mask = (j <= i) & (j >= i - WINDOW)
        scale = 1.0 / np.sqrt(HEAD_DIM)
        scores = jnp.einsum('bhid,bhjd->bhij', q, k) * scale
        scores = jnp.where(mask, scores, jnp.finfo(scores.dtype).min)
        attn = jax.nn.softmax(scores, axis=-1)
        out = jnp.einsum('bhij,bhjd->bhid', attn, v)
        out = jnp.moveaxis(out, 1, 2).reshape(b, l, e)
        return jnp.einsum('ble,ef->blf', out, W_out) + b_out

    def _L0_ffn_ref(x, W_up, W_gate, W_down):
        import jax, jax.numpy as jnp
        import numpy as np
        D_MODEL = 512
        D_EXPERT = 2048
        EPS = 1e-08

        def ternary_quant(w):
            scale = jnp.mean(jnp.abs(w)) + EPS
            q = jnp.clip(jnp.round(w / scale), -1.0, 1.0) * scale
            return w + jax.lax.stop_gradient(q - w)
        wu = ternary_quant(W_up)
        wg = ternary_quant(W_gate)
        wd = ternary_quant(W_down)
        up = jnp.einsum('bsd,ed->bse', x, wu)
        gate = jnp.einsum('bsd,ed->bse', x, wg)
        hidden = jax.nn.silu(up) * gate
        return jnp.einsum('bse,de->bsd', hidden, wd)
    x = L0_attn_x
    x = x + _layernorm(_L0_attn_ref(_layernorm(x, axis=-1), L0_attn_W_qkv, L0_attn_W_out, L0_attn_b_out), axis=-1)
    x = x + _layernorm(_L0_ffn_ref(_layernorm(x, axis=-1), L0_ffn_W_up, L0_ffn_W_gate, L0_ffn_W_down), axis=-1)
    return x

_drawn_inputs = setup_inputs


def setup_inputs(seed=0):
    import zlib

    import numpy as np

    out = dict(_drawn_inputs(seed))
    spreads = {}
    factors = {}
    for name, (base, spread) in spreads.items():
        noise = np.random.default_rng([zlib.crc32(name.encode()), seed]).standard_normal(out[name].shape)
        drawn = base * np.exp(spread * noise) if base else spread * noise
        out[name] = jnp.asarray(drawn.astype(out[name].dtype))
    for name, factor in factors.items():
        out[name] = (out[name] * factor).astype(out[name].dtype)
    return out
```

```python
from contextlib import ExitStack

import numpy as np

import concourse.bass as bass
from concourse import mybir

P = 128
F32 = mybir.dt.float32
F16 = mybir.dt.float16
I32 = mybir.dt.int32
ALU = mybir.AluOpType
ACT = mybir.ActivationFunctionType
AX = mybir.AxisListType

D = 512
H = 16
HD = D // H
WINDOW = P
F = 2048
BATCH, SEQ = 2, 2048
TOK = BATCH * SEQ
MT = 512
NM = TOK // MT
TT = MT // P
DC = D // P
NG = H // 4
STEPS = TT * 2
UNITS = NG * STEPS
PER_BATCH = SEQ // MT
EPS = 1e-5

QKV_SCALE = 32.0
P_SCALE = 2.0 ** 14
XN_SCALE = 2.0 ** 10
H_SCALE = 2.0 ** -3
NEG = -1.0e38


FILLER = [
    [("Q", 1, (0, 1, 2))],
    [("Q", 1, (3,)), ("K", 1, (0, 1))],
    [("K", 1, (2, 3)), ("OT", 3, ())],
    [("V", 1, (0, 1, 2))],
    [("V", 1, (3,)), ("Y", 0, (0, 1))],
    [("Y", 0, (2, 3)), ("Y", 1, (0,))],
    [("Y", 1, (1, 2, 3))],
    [("VT", 1, ())],
    [("Q", 2, (0, 1, 2))],
    [("Q", 2, (3,)), ("K", 2, (0, 1))],
    [("K", 2, (2, 3)), ("Y", 2, (0,))],
    [("Y", 2, (1, 2, 3))],
    [("V", 2, (0, 1, 2))],
    [("V", 2, (3,)), ("Y", 3, (0,))],
    [("Y", 3, (1, 2, 3))],
    [("VT", 2, ())],
    [("OT", 0, ()), ("Q", 3, (0, 1))],
    [("Q", 3, (2, 3))],
    [("K", 3, (0, 1)), ("OT", 1, ())],
    [("K", 3, (2, 3))],
    [("V", 3, (0, 1, 2))],
    [("V", 3, (3,)), ("T", 0, ())],
    [("T", 1, ()), ("T", 2, ())],
    [("T", 3, ()), ("VT", 3, ())],
    [("Q", 0, (0, 1))],
    [("Q", 0, (2, 3))],
    [("K", 0, (0, 1)), ("OT", 2, ())],
    [("K", 0, (2, 3))],
    [("V", 0, (0, 1, 2))],
    [("V", 0, (3,))],
    [],
    [("VT", 0, ())],
]
BEFORE = [("T", k) for k in range(DC)] + [("Q", 0), ("K", 0), ("V", 0), ("VT", 0)]
AFTER = [("OT", 3)] + [("Y", t) for t in range(TT)]


class Plan:

    def __init__(self, of_previous, of_next):
        def kept(job):
            if job[0] == "Y" or job == ("OT", 3):
                return of_previous
            return of_next or not (job[0] == "T" or job[0] in ("Q", "K", "V", "VT") and job[1] == 0)

        self.steps = [[p for p in step if kept(p[:2])] for step in FILLER]
        self.jobs = []
        self.ends = [[] for _ in self.steps]
        for step in self.steps:
            for kind, idx, _ in step:
                if (kind, idx) not in self.jobs:
                    self.jobs.append((kind, idx))
        for job in self.jobs:
            self.ends[max(s for s, step in enumerate(self.steps) for p in step if p[:2] == job)].append(job)


FIRST, MIDDLE, LAST = Plan(False, True), Plan(True, True), Plan(True, False)
assert len(MIDDLE.jobs) % 2 == 0 and FIRST.jobs[-2:] == MIDDLE.jobs[-2:]


def jobs_before(plan, i):
    if plan is FIRST:
        return len(BEFORE)
    return len(BEFORE) + len(FIRST.jobs) - len(MIDDLE.jobs) + i * len(MIDDLE.jobs)


def bank_of(plan, n):
    return (len(BEFORE) + (0 if plan is FIRST else len(FIRST.jobs)) + n) % 2


def tile_of(job, i):
    kind, idx = job
    if kind == "Y" or job == ("OT", 3):
        return i - 1
    if kind == "T" or kind in ("Q", "K", "V", "VT") and idx == 0:
        return i + 1
    return i


def at_least(engine, semaphore, value):
    if isinstance(value, int) and value <= 0:
        return
    engine.wait_ge(semaphore, value)


def worked_out(engine, *values):
    return [v if isinstance(v, int) else engine.snap(engine.to_reg(v)) for v in values]


def settled(engine, semaphore):
    engine.wait_ge(semaphore, 1)


def layer(nc, x, w_qkv, w_out, b_out, w_up, w_gate, w_down, cos_t, sin_t, bands, ident_in, out):
    with ExitStack() as whole:
        X = whole.enter_context(nc.sbuf_tensor("X", [P, NM * TT, D], F32))
        ident = whole.enter_context(nc.sbuf_tensor("ident", [P, P], F32))
        minus_half = whole.enter_context(nc.sbuf_tensor("minus_half", [P, TT], F32))
        attention(nc, X, ident, minus_half, x, w_qkv, w_out, b_out, cos_t, sin_t, bands, ident_in)
        ffn(nc, X, ident, minus_half, w_up, w_gate, w_down, out)


def attention(nc, X, ident, minus_half, x, w_qkv, w_out, b_out, cos_t, sin_t, bands, ident_in):
    with ExitStack() as ctx:
        def sb(name, shape, dt=F32):
            return ctx.enter_context(nc.sbuf_tensor(name, shape, dt))

        def ps(name):
            return ctx.enter_context(nc.psum_tensor(name, [P, 512], F32))

        def sem(name):
            return ctx.enter_context(nc.semaphore(name))

        W = sb("W", [P, 3, DC, D])
        Wo = sb("Wo", [P, DC, D])
        bias_bc = sb("bias_bc", [P, D])
        cosT = sb("cosT", [P, MT])
        sinT = sb("sinT", [P, MT])
        band = sb("band", [P, 2 * P])
        band0 = sb("band0", [P, 2 * P])
        xn = sb("xn", [P, TT, D])
        xnT = sb("xnT", [P, DC, MT])
        st_x = sb("st_x", [P, TT, 6])
        mv_x = sb("mv_x", [P, TT, 2])
        var_x = sb("var_x", [P, TT])
        rstd_x = sb("rstd_x", [P, TT])
        st_y = sb("st_y", [P, TT, 6])
        mv_y = sb("mv_y", [P, TT, 2])
        var_y = sb("var_y", [P, TT])
        rstd_y = sb("rstd_y", [P, TT])
        rot = sb("rot", [P, 2, MT])
        swp = sb("swp", [P, 2, MT])
        r_hi = sb("r_hi", [P, 2, MT], F16)
        r_lo = sb("r_lo", [P, 2, MT], F16)
        Qp = sb("Qp", [P, 2, 4, MT], F16)
        Kp = sb("Kp", [P, 2, 4, MT], F16)
        Kc = sb("Kc", [P, H, P], F16)
        vT = sb("vT", [P, MT])
        Vp = sb("Vp", [P, 2, TT, 4, 2 * HD], F16)
        Vc = sb("Vc", [P, H, 2 * HD], F16)
        prob = sb("prob", [P, 2, 2, 2 * P])
        peak = sb("peak", [P, 2, 2])
        rsum = sb("rsum", [P, 2, 4])
        rinv = sb("rinv", [P, 2, 4])
        p_hi = sb("p_hi", [P, 2, 4, P], F16)
        p_lo = sb("p_lo", [P, 2, 4, P], F16)
        o_raw = sb("o_raw", [P, 2, 4, HD])
        o_n = sb("o_n", [P, 2, TT, 4, HD])
        oT = sb("oT", [P, NG, MT])
        y_sb = sb("y_sb", [P, TT, D])
        z_sb = sb("z_sb", [P, TT, D])
        wmax, wmax_all, p2, p2_inv, p2_sq = (sb(n, [P, 1]) for n in ("wmax", "wmax_all", "p2", "p2_inv", "p2_sq"))
        p2_bits = sb("p2_bits", [P, 1], I32)
        w_scale, neg_score_scale, o_scale = (sb(n, [P, 1]) for n in ("w_scale", "neg_score_scale", "o_scale"))

        S_ps = [ps("S0"), ps("S1")]
        PT_ps = [ps("PT0"), ps("PT1")]
        O_ps = [ps("O0"), ps("O1")]
        J_ps = [ps("J0"), ps("J1")]

        x0_in, x1_in, x_rest_in, w_in, wo_in = sem("x0_in"), sem("x1_in"), sem("x_rest_in"), sem("w_in"), sem("wo_in")
        const_in, bias_in, table_in, band0_in = sem("const_in"), sem("bias_in"), sem("table_in"), sem("band0_in")
        q_packed, k_packed = sem("q_packed"), sem("k_packed")
        set_up, wmax_done, wmax_spread, scales, w_scaled = (
            sem("set_up"), sem("wmax_done"), sem("wmax_spread"), sem("scales"), sem("w_scaled"))
        score_done, logit_done, exp_done, pt_done = sem("score_done"), sem("logit_done"), sem("exp_done"), sem("pt_done")
        p_hi_done, p_lo_done, av_done = sem("p_hi_done"), sem("p_lo_done"), sem("av_done")
        o_read, o_inv, o_norm = sem("o_read"), sem("o_inv"), sem("o_norm")
        job_full = sem("job_full")
        cos_done, swap_done, vT_done, v_hi_done, v_lo_done = (
            sem("cos_done"), sem("swap_done"), sem("vT_done"), sem("v_hi_done"), sem("v_lo_done"))
        xnT_done, oT_done, y_copied = sem("xnT_done"), sem("oT_done"), sem("y_copied")
        sin_done, rot_done, r_hi_done, r_lo_done = sem("sin_done"), sem("rot_done"), sem("r_hi_done"), sem("r_lo_done")
        k_carried, v_carried = sem("k_carried"), sem("v_carried")
        x_stats, x_mv, x_var, x_rstd, xn_done = sem("x_stats"), sem("x_mv"), sem("x_var"), sem("x_rstd"), sem("xn_done")
        y_stats, y_mv, y_var, y_rstd = sem("y_stats"), sem("y_mv"), sem("y_var"), sem("y_rstd")
        z_done, x1_done = sem("z_done"), sem("x1_done")

        def emptied(engine, job, i):
            kind, idx = job
            i = tile_of(job, i)
            if kind in ("Q", "K"):
                at_least(engine, swap_done, 2 * (i * NG + idx) + (1 if kind == "Q" else 2))
            elif kind == "V":
                at_least(engine, vT_done, i * NG + idx + 1)
            elif kind == "VT":
                at_least(engine, v_lo_done, i * NG + idx + 1)
            elif kind == "OT":
                at_least(engine, oT_done, i * NG + idx + 1)
            elif kind == "T":
                at_least(engine, xnT_done, i * DC + idx + 1)
            elif kind == "Y":
                at_least(engine, y_copied, i * TT + idx + 1)

        block = ctx.enter_context(nc.Block())

        @block.sync
        def _(sp):
            x_tiles = x.rearrange("b (n p) d -> p (b n) d", p=P)
            sp.dma_start(X[:, 0:TT, :], x_tiles[:, 0:TT, :]).then_inc(x0_in, 16)
            sp.dma_start(W[:], w_qkv.rearrange("s (c p) n -> p s c n", p=P)).then_inc(w_in, 16)
            sp.dma_start(ident[:], ident_in).then_inc(const_in, 16)
            sp.dma_start(band[:], bands[1]).then_inc(const_in, 16)
            sp.dma_start(cosT[:], cos_t[0]).then_inc(table_in, 16)
            sp.dma_start(sinT[:], sin_t[0]).then_inc(table_in, 16)
            sp.dma_start(band0[:], bands[0]).then_inc(band0_in, 16)
            sp.dma_start(X[:, TT:2 * TT, :], x_tiles[:, TT:2 * TT, :]).then_inc(x1_in, 16)
            sp.dma_start(Wo[:], w_out.rearrange("(c p) n -> p c n", p=P)).then_inc(wo_in, 16)
            sp.dma_start(bias_bc[:], b_out.rearrange("(a n) -> a n", a=1).to_broadcast([P, D])).then_inc(bias_in, 16)
            sp.dma_start(X[:, 2 * TT:, :], x_tiles[:, 2 * TT:, :]).then_inc(x_rest_in, 16)

            def pack(i, g):
                n = i * NG + g
                q_split, k_split, scores, carried = worked_out(
                    sp, 2 * n + 1, 2 * n + 2, (n - 1) * STEPS, n - 1)
                sp.wait_ge(r_lo_done, q_split)
                at_least(sp, score_done, scores)
                for part, src in enumerate((r_hi, r_hi, r_lo, r_lo)):
                    for h in range(4):
                        sp.dma_start(Qp[part * HD:(part + 1) * HD, g % 2, h, :],
                                     src[h * HD:(h + 1) * HD, 0, :]).then_inc(q_packed, 16)
                sp.wait_ge(r_lo_done, k_split)
                at_least(sp, k_carried, carried)
                for part, src in enumerate((r_hi, r_lo, r_hi, r_lo)):
                    for h in range(4):
                        sp.dma_start(Kp[part * HD:(part + 1) * HD, g % 2, h, :],
                                     src[h * HD:(h + 1) * HD, 1, :]).then_inc(k_packed, 16)

            def macro_tile(i, plan):
                for g in range(1, NG):
                    pack(i, g)
                if plan is LAST:
                    return
                rotations, next_tile = worked_out(sp, 2 * NG * (i + 1), i + 1)
                used = worked_out(sp, i * UNITS + (NG - 1) * STEPS + 2)[0]
                sp.wait_ge(cos_done, rotations)
                sp.wait_ge(sin_done, rotations)
                sp.dma_start(cosT[:], row(cos_t, next_tile)).then_inc(table_in, 16)
                sp.dma_start(sinT[:], row(sin_t, next_tile)).then_inc(table_in, 16)
                sp.wait_ge(logit_done, used)
                sp.dma_start(band0[:], row(bands, next_tile)).then_inc(band0_in, 16)
                pack(i + 1, 0)

            def row(t, n):
                return t[bass.ds(n, 1)].rearrange("a p k -> (a p) k")

            pack(0, 0)
            macro_tile(0, FIRST)
            with sp.Fori(1, NM - 1) as i:
                macro_tile(i, MIDDLE)
            macro_tile(NM - 1, LAST)

        @block.gpsimd
        def _(pool):
            pool.memset(minus_half[:], -0.5).then_inc(set_up, 1)
            pool.memset(Kc[:], 0.0).then_inc(set_up, 1)
            pool.memset(Vc[:], 0.0).then_inc(set_up, 1)
            pool.wait_ge(set_up, 3)

            def rstd_of_x(i):
                moments = worked_out(pool, TT * (i + 1))[0]
                settled(pool, set_up)
                pool.wait_ge(x_mv, moments)
                pool.tensor_scalar(var_x[:], mv_x[:, :, 1], EPS, None, ALU.add).then_inc(x_var, 1)
                pool.wait_ge(x_var, i + 1)
                pool.tensor_tensor(rstd_x[:], var_x[:], minus_half[:], ALU.pow).then_inc(x_rstd, 1)

            def rstd_of_y(i):
                moments = worked_out(pool, TT * (i + 1))[0]
                settled(pool, set_up)
                pool.wait_ge(y_mv, moments)
                pool.tensor_scalar(var_y[:], mv_y[:, :, 1], EPS, None, ALU.add).then_inc(y_var, 1)
                pool.wait_ge(y_var, i + 1)
                pool.tensor_tensor(rstd_y[:], var_y[:], minus_half[:], ALU.pow).then_inc(y_rstd, 1)

            def rotate(i, g):
                for a, packed in enumerate((q_packed, k_packed)):
                    n = 2 * (i * NG + g) + a
                    pool.wait_ge(swap_done, n + 1)
                    pool.tensor_tensor(swp[:, a, :], swp[:, a, :], sinT[:], ALU.mult).then_inc(sin_done, 1)
                    pool.wait_ge(cos_done, n + 1)
                    pool.wait_ge(sin_done, n + 1)
                    pool.tensor_tensor(rot[:, a, :], rot[:, a, :], swp[:, a, :], ALU.add).then_inc(rot_done, 1)
                    rotated, landed = worked_out(pool, n + 1, 256 * (i * NG + g))
                    settled(pool, set_up)
                    pool.wait_ge(rot_done, rotated)
                    at_least(pool, packed, landed)
                    pool.tensor_copy(r_hi[:, a, :], rot[:, a, :]).then_inc(r_hi_done, 1)
                    pool.wait_ge(r_hi_done, n + 1)
                    pool.tensor_tensor(r_lo[:, a, :], rot[:, a, :], r_hi[:, a, :], ALU.subtract).then_inc(r_lo_done, 1)

            def residual(i):
                for t in range(TT):
                    pool.wait_ge(z_done, TT * i + t + 1)
                    row = X[:, bass.ds(i * TT + t, 1), :]
                    pool.tensor_tensor(row, row, z_sb[:, t:t + 1, :], ALU.add).then_inc(x1_done, 1)

            def macro_tile(i, plan):
                rotate(i, 1)
                rotate(i, 2)
                if plan is not LAST:
                    rstd_of_x(i + 1)
                if plan is not FIRST:
                    rstd_of_y(i - 1)
                rotate(i, 3)
                if plan is not FIRST:
                    residual(i - 1)
                if plan is not LAST:
                    rotate(i + 1, 0)

            rstd_of_x(0)
            pool.wait_ge(wmax_done, 1)
            pool.partition_all_reduce(wmax_all[:], wmax[:], P, bass.bass_isa.ReduceOp.max).then_inc(wmax_spread, 1)
            rotate(0, 0)
            macro_tile(0, FIRST)
            with pool.Fori(1, NM - 1) as i:
                macro_tile(i, MIDDLE)
            macro_tile(NM - 1, LAST)
            rstd_of_y(NM - 1)
            residual(NM - 1)

        @block.scalar
        def _(act):
            def empty(job, i, number, bank):
                kind, g = job
                n = tile_of(job, i) * NG + g
                if kind == "V":
                    act.wait_ge(job_full, number + 1)
                    nc.scalar.activation(vT[:], J_ps[bank][:], ACT.Copy).then_inc(vT_done, 1)
                elif kind == "VT":
                    act.wait_ge(job_full, number + 1)
                    at_least(act, av_done, (n - 1) * STEPS)
                    at_least(act, v_carried, n - 1)
                    nc.scalar.activation(Vp[:, g % 2, :, :, 0:HD],
                                         J_ps[bank][:].rearrange("p (t h d) -> p t h d", t=TT, h=4),
                                         ACT.Copy).then_inc(v_hi_done, 1)
                elif kind == "OT":
                    act.wait_ge(job_full, number + 1)
                    nc.scalar.activation(oT[:, g, :], J_ps[bank][:], ACT.Copy).then_inc(oT_done, 1)
                elif kind == "T":
                    act.wait_ge(job_full, number + 1)
                    nc.scalar.activation(xnT[:, g, :], J_ps[bank][:], ACT.Copy).then_inc(xnT_done, 1)

            def exp(i, u):
                act.wait_ge(logit_done, i * UNITS + u + 1)
                if u % 2 == 0:
                    at_least(act, o_inv, i * (UNITS // 2) + u // 2 - 1)
                for h in range(2):
                    col = 2 * (u % 2) + h
                    e = nc.scalar.activation(prob[:, u % 2, h, :], prob[:, u % 2, h, :], ACT.Exp,
                                             bias=peak[:, u % 2, h:h + 1], scale=-1.0,
                                             accum_out=rsum[:, u // 2 % 2, col:col + 1])
                e.then_inc(exp_done, 1)

            def p_high(i, u):
                act.wait_ge(pt_done, i * UNITS + u + 1)
                at_least(act, av_done, i * UNITS + u - 1)
                nc.scalar.activation(p_hi[:, u % 2, :, :],
                                     PT_ps[u % 2][:].rearrange("p (a k) -> p a k", a=4),
                                     ACT.Copy, scale=P_SCALE).then_inc(p_hi_done, 1)

            def macro_tile(i, plan):
                for u in range(UNITS):
                    if u + 1 < UNITS or plan is not LAST:
                        exp(i, u + 1)
                    for job in plan.ends[u]:
                        n = plan.jobs.index(job)
                        empty(job, i, jobs_before(plan, i) + n, bank_of(plan, n))
                    p_high(i, u)

            for n, job in enumerate(BEFORE):
                empty(job, -1, n, n % 2)
            exp(0, 0)
            macro_tile(0, FIRST)
            with act.Fori(1, NM - 1) as i:
                macro_tile(i, MIDDLE)
            macro_tile(NM - 1, LAST)
            done = jobs_before(LAST, NM - 1) + len(LAST.jobs)
            empty(AFTER[0], NM, done, done % 2)

        @block.vector
        def _(dve):
            def layer_norm_stats(i, t):
                x_row = X[:, bass.ds(i * TT + t, 1), :]
                nc.vector.bn_stats(st_x[:, t, :], x_row).then_inc(x_stats, 1)

            def layer_norm_moments(i):
                counts = worked_out(dve, *(i * TT + t + 1 for t in range(TT)))
                for t in range(TT):
                    settled(dve, x0_in)
                    dve.wait_ge(x_stats, counts[t])
                    nc.vector.bn_aggr(mv_x[:, t, :], st_x[:, t, :]).then_inc(x_mv, 1)

            def layer_norm(i, t):
                dve.wait_ge(x_rstd, i + 1)
                x_row = X[:, bass.ds(i * TT + t, 1), :]
                nc.vector.tensor_scalar(xn[:, t:t + 1, :], x_row, mv_x[:, t, 0:1], rstd_x[:, t:t + 1],
                                        ALU.subtract, ALU.mult).then_inc(xn_done, 1)

            def empty(job, i, number, bank):
                kind, g = job
                tile = tile_of(job, i)
                n = tile * NG + g
                if kind in ("Q", "K"):
                    a = 0 if kind == "Q" else 1
                    dve.wait_ge(job_full, number + 1)
                    dve.wait_ge(table_in, 32 * (tile + 1))
                    at_least(dve, r_lo_done, 2 * n + a - 1)
                    nc.vector.tensor_tensor(rot[:, a, :], J_ps[bank][:], cosT[:], ALU.mult).then_inc(cos_done, 1)
                    nc.vector.stream_shuffle(swp[:, a, :], J_ps[bank][:],
                                             [d ^ 1 for d in range(HD)]).then_inc(swap_done, 1)
                elif kind == "VT":
                    dve.wait_ge(v_hi_done, n + 1)
                    nc.vector.tensor_tensor(Vp[:, g % 2, :, :, HD:2 * HD],
                                            J_ps[bank][:].rearrange("p (t h d) -> p t h d", t=TT, h=4),
                                            Vp[:, g % 2, :, :, 0:HD], ALU.subtract).then_inc(v_lo_done, 1)
                elif kind == "Y":
                    dve.wait_ge(job_full, number + 1)
                    nc.vector.tensor_tensor(y_sb[:, g, :], J_ps[bank][:], bias_bc[:], ALU.add).then_inc(y_copied, 1)

            def logits(i, u):
                first_tile = u // 2 % TT == 0
                scored, transposed, bands_in = worked_out(
                    dve, i * UNITS + u + 1, i * UNITS + u - 1, 16 * (i + 1 + u // UNITS))
                settled(dve, x0_in)
                dve.wait_ge(score_done, scored)
                at_least(dve, pt_done, transposed)
                if first_tile and u % 2 == 0:
                    dve.wait_ge(band0_in, bands_in)
                for h in range(2):
                    e = nc.vector.tensor_tensor_reduce(
                        out=prob[:, u % 2, h, :], in0=S_ps[u % 2][:, h * 2 * P:(h + 1) * 2 * P],
                        in1=(band0 if first_tile else band)[:], scale=neg_score_scale[:], scalar=3.0e38,
                        op0=ALU.add, op1=ALU.min, accum_out=peak[:, u % 2, h:h + 1])
                e.then_inc(logit_done, 1)

            def p_low(i, u):
                dve.wait_ge(p_hi_done, i * UNITS + u + 1)
                at_least(dve, av_done, i * UNITS + u - 1)
                nc.vector.scalar_tensor_tensor(p_lo[:, u % 2, :, :],
                                               PT_ps[u % 2][:].rearrange("p (a k) -> p a k", a=4), P_SCALE,
                                               p_hi[:, u % 2, :, :], ALU.mult, ALU.subtract).then_inc(p_lo_done, 1)

            def normalise(i, k, ot_full):
                tile = i * (UNITS // 2) + k
                g, t = k // TT, k % TT
                dve.wait_ge(av_done, 2 * tile + 2)
                nc.vector.tensor_reduce(
                    o_raw[:, k % 2, :, :],
                    O_ps[k % 2][:, 0:4 * 2 * HD].rearrange("p (h s d) -> p h d s", h=4, s=2),
                    AX.X, ALU.add).then_inc(o_read, 1)
                nc.vector.reciprocal(rinv[:, k % 2, :], rsum[:, k % 2, :]).then_inc(o_inv, 1)
                dve.wait_ge(o_read, tile + 1)
                dve.wait_ge(o_inv, tile + 1)
                at_least(dve, job_full, ot_full)
                nc.vector.scalar_tensor_tensor(
                    o_n[:, g % 2, t, :, :], o_raw[:, k % 2, :, :], o_scale[:],
                    rinv[:, k % 2, :].unsqueeze(2).to_broadcast([P, 4, HD]), ALU.mult, ALU.mult).then_inc(o_norm, 1)

            def carry_k(i, g):
                dve.wait_ge(score_done, (i * NG + g) * STEPS + 2)
                nc.vector.tensor_copy(Kc[:, 4 * g:4 * g + 4, :], Kp[:, g % 2, :, MT - P:MT]).then_inc(k_carried, 1)

            def carry_v(i, g):
                dve.wait_ge(av_done, (i * NG + g) * STEPS + 2)
                nc.vector.tensor_copy(Vc[:, 4 * g:4 * g + 4, :], Vp[:, g % 2, TT - 1, :, :]).then_inc(v_carried, 1)

            def y_statistics(i, t):
                dve.wait_ge(y_copied, i * TT + t + 1)
                nc.vector.bn_stats(st_y[:, t, :], y_sb[:, t, :]).then_inc(y_stats, 1)

            def y_moments(i):
                counts = worked_out(dve, *(i * TT + t + 1 for t in range(TT)))
                for t in range(TT):
                    settled(dve, x0_in)
                    dve.wait_ge(y_stats, counts[t])
                    nc.vector.bn_aggr(mv_y[:, t, :], st_y[:, t, :]).then_inc(y_mv, 1)

            def y_normalise(i, t):
                dve.wait_ge(y_rstd, i + 1)
                nc.vector.tensor_scalar(z_sb[:, t, :], y_sb[:, t, :], mv_y[:, t, 0:1], rstd_y[:, t:t + 1],
                                        ALU.subtract, ALU.mult).then_inc(z_done, 1)

            def ot_number(i, plan, g):
                if g == 0:
                    if plan is FIRST:
                        return 0
                    before = FIRST.jobs if plan is FIRST else MIDDLE.jobs
                    return jobs_before(plan, i) - len(before) + before.index(("OT", 2)) + 1
                job = ("OT", 3) if g == 1 else ("OT", g - 2)
                return jobs_before(plan, i) + plan.jobs.index(job) + 1 if job in plan.jobs else 0

            def macro_tile(i, plan):
                for u in range(UNITS):
                    g, s = u // STEPS, u % STEPS
                    if u + 1 < UNITS or plan is not LAST:
                        logits(i, u + 1)
                    for job in plan.ends[u]:
                        n = plan.jobs.index(job)
                        empty(job, i, jobs_before(plan, i) + n, bank_of(plan, n))
                    p_low(i, u)
                    if u % 2 == 0 and u > 0:
                        normalise(i, u // 2 - 1, ot_number(i, plan, (u // 2 - 1) // TT))
                    if u == 0 and plan is not FIRST:
                        last_tile = UNITS // 2 - 1
                        before = FIRST if plan is FIRST else MIDDLE
                        normalise(i - 1, last_tile, jobs_before(plan, i) - len(before.jobs) + before.jobs.index(("OT", 1)) + 1)
                    if s == 3:
                        carry_k(i, g)
                    if s == 5:
                        carry_v(i, g)
                    if plan is not LAST:
                        if u in (8, 9, 10, 11):
                            if u == 8:
                                dve.wait_ge(x1_in if plan is FIRST else x_rest_in, 16)
                            layer_norm_stats(i + 1, u - 8)
                        if u == 12:
                            layer_norm_moments(i + 1)
                        if u in (16, 17, 18, 19):
                            layer_norm(i + 1, u - 16)
                    if plan is not FIRST:
                        for kind, t in (plan.ends[u - 1] if u else []):
                            if kind == "Y":
                                y_statistics(i - 1, t)
                        if u == 15:
                            y_moments(i - 1)
                        if u in (20, 21, 22, 23):
                            y_normalise(i - 1, u - 20)

            dve.wait_ge(x0_in, 16)
            for t in range(TT):
                layer_norm_stats(0, t)
            layer_norm_moments(0)
            for t in range(TT):
                layer_norm(0, t)
            dve.wait_ge(w_in, 16)
            nc.vector.tensor_reduce(wmax[:], W[:].rearrange("p s c n -> p (s c n)"), AX.X, ALU.max,
                                    apply_absolute_value=True).then_inc(wmax_done, 1)
            dve.wait_ge(wmax_spread, 1)
            nc.vector.tensor_scalar(p2_bits[:], wmax_all[:].bitcast(I32), 0x7F800000, None,
                                    ALU.bitwise_and).then_inc(scales, 1)
            dve.wait_ge(scales, 1)
            nc.vector.tensor_scalar(p2[:], p2_bits[:].bitcast(F32), 2.0 ** -33, None, ALU.max).then_inc(scales, 1)
            dve.wait_ge(scales, 2)
            nc.vector.reciprocal(p2_inv[:], p2[:]).then_inc(scales, 1)
            nc.vector.tensor_tensor(p2_sq[:], p2[:], p2[:], ALU.mult).then_inc(scales, 1)
            nc.vector.tensor_scalar(o_scale[:], p2[:], 1.0 / (QKV_SCALE * P_SCALE), None, ALU.mult).then_inc(scales, 1)
            dve.wait_ge(scales, 4)
            nc.vector.tensor_scalar(w_scale[:], p2_inv[:], QKV_SCALE, None, ALU.mult).then_inc(scales, 1)
            nc.vector.tensor_scalar(neg_score_scale[:], p2_sq[:], -float(np.float32(HD ** -0.5)) / QKV_SCALE ** 2,
                                    None, ALU.mult).then_inc(scales, 1)
            dve.wait_ge(scales, 7)
            for s in range(3):
                nc.vector.tensor_scalar(W[:, s], W[:, s], w_scale[:], None, ALU.mult).then_inc(w_scaled, 1)
            dve.wait_ge(const_in, 32)
            dve.wait_ge(bias_in, 16)
            dve.wait_ge(set_up, 3)
            for n, job in enumerate(BEFORE):
                empty(job, -1, n, n % 2)
            logits(0, 0)
            macro_tile(0, FIRST)
            with dve.Fori(1, NM - 1) as i:
                macro_tile(i, MIDDLE)
            macro_tile(NM - 1, LAST)
            i = NM - 1
            normalise(i, UNITS // 2 - 1, jobs_before(LAST, i) + LAST.jobs.index(("OT", 1)) + 1)
            done = jobs_before(LAST, i) + len(LAST.jobs)
            for n, job in enumerate(AFTER):
                empty(job, NM, done + n, (done + n) % 2)
                if job[0] == "Y":
                    y_statistics(i, job[1])
            y_moments(i)
            for t in range(TT):
                y_normalise(i, t)

        @block.tensor
        def _(pe):
            def score(i, u):
                g, t, pair = u // STEPS % NG, u // 2 % TT, u % 2
                if u % STEPS == 0:
                    n = i * NG + u // STEPS
                    pe.wait_ge(q_packed, 256 * (n + 1))
                    pe.wait_ge(k_packed, 256 * (n + 1))
                at_least(pe, logit_done, i * UNITS + u - 1)
                for h in range(2):
                    head = 2 * pair + h
                    q = Qp[:, g % 2, head, t * P:(t + 1) * P]
                    at = h * 2 * P
                    if t == 0:
                        pe.matmul(S_ps[u % 2][:, at:at + P], q, Kc[:, 4 * g + head, :], start=True, stop=True)
                        e = pe.matmul(S_ps[u % 2][:, at + P:at + 2 * P], q, Kp[:, g % 2, head, 0:P],
                                      start=True, stop=True)
                    else:
                        e = pe.matmul(S_ps[u % 2][:, at:at + 2 * P], q, Kp[:, g % 2, head, (t - 1) * P:(t + 1) * P],
                                      start=True, stop=True)
                e.then_inc(score_done, 1)

            def transpose_probs(i, u):
                pe.wait_ge(exp_done, i * UNITS + u + 1)
                at_least(pe, p_lo_done, i * UNITS + u - 1)
                for a in range(4):
                    e = pe.transpose(PT_ps[u % 2][:, a * P:(a + 1) * P],
                                     prob[:, u % 2, a // 2, (a % 2) * P:(a % 2 + 1) * P], ident[:])
                e.then_inc(pt_done, 1)

            def weighted_values(i, u):
                g, t, pair = u // STEPS, u // 2 % TT, u % 2
                tile = i * (UNITS // 2) + u // 2
                if u % STEPS == 0:
                    pe.wait_ge(v_lo_done, i * NG + g + 1)
                pe.wait_ge(p_lo_done, i * UNITS + u + 1)
                if pair == 0:
                    at_least(pe, o_read, tile - 1)
                for h in range(2):
                    head = 2 * pair + h
                    dst = O_ps[u // 2 % 2][:, head * 2 * HD:(head + 1) * 2 * HD]
                    for n, (key_tile, part) in enumerate(((0, p_hi), (1, p_hi), (0, p_lo), (1, p_lo))):
                        if t == 0 and key_tile == 0:
                            v = Vc[:, 4 * g + head, :]
                        else:
                            v = Vp[:, g % 2, t - 1 + key_tile, head, :]
                        e = pe.matmul(dst, part[:, u % 2, 2 * h + key_tile, :], v, start=(n == 0), stop=(n == 3))
                e.then_inc(av_done, 1)

            def work(piece, i, bank):
                kind, g, chunks = piece
                i = tile_of((kind, g), i)
                dst = J_ps[bank]
                e = None
                if kind in ("Q", "K", "V"):
                    s = "QKV".index(kind)
                    if 0 in chunks:
                        pe.wait_ge(xnT_done, DC * (i + 1))
                    for c in chunks:
                        e = pe.matmul(dst[:], W[:, s, c, g * P:(g + 1) * P], xnT[:, c, :],
                                      start=(c == 0), stop=(c == DC - 1))
                    return e if DC - 1 in chunks else None
                if kind == "Y":
                    if 0 in chunks:
                        pe.wait_ge(oT_done, NG * (i + 1))
                    for c in chunks:
                        e = pe.matmul(dst[:], oT[:, c, g * P:(g + 1) * P], Wo[:, c, :],
                                      start=(c == 0), stop=(c == NG - 1))
                    return e if NG - 1 in chunks else None
                if kind == "VT":
                    pe.wait_ge(vT_done, i * NG + g + 1)
                    src = [vT[:, t * P:(t + 1) * P] for t in range(TT)]
                elif kind == "OT":
                    pe.wait_ge(o_norm, (i * NG + g + 1) * TT)
                    src = [o_n[:, g % 2, t].rearrange("p h d -> p (h d)") for t in range(TT)]
                else:
                    pe.wait_ge(xn_done, (i + 1) * TT)
                    src = [xn[:, t, g * P:(g + 1) * P] for t in range(TT)]
                for t in range(TT):
                    e = pe.transpose(dst[:, t * P:(t + 1) * P], src[t], ident[:])
                return e

            def fill(piece, i, plan):
                n = plan.jobs.index(piece[:2])
                if 0 in piece[2] or not piece[2]:
                    if n >= 2:
                        emptied(pe, plan.jobs[n - 2], i)
                    elif plan is FIRST:
                        emptied(pe, BEFORE[n - 2], -1)
                    else:
                        emptied(pe, MIDDLE.jobs[n - 2], i - 1)
                e = work(piece, i, bank_of(plan, n))
                if e is not None:
                    e.then_inc(job_full, 1)

            def macro_tile(i, plan):
                for u in range(UNITS):
                    if u + 1 < UNITS or plan is not LAST:
                        score(i, u + 1)
                    for piece in plan.steps[u]:
                        fill(piece, i, plan)
                    transpose_probs(i, u)
                    if u > 0:
                        weighted_values(i, u - 1)
                    elif plan is not FIRST:
                        weighted_values(i - 1, UNITS - 1)

            pe.wait_ge(const_in, 32)
            pe.wait_ge(w_scaled, 3)
            pe.wait_ge(set_up, 3)
            pe.wait_ge(wo_in, 16)
            whole_jobs = {"Q": (0, 1, 2, 3), "K": (0, 1, 2, 3), "V": (0, 1, 2, 3), "Y": (0, 1, 2, 3)}
            for n, job in enumerate(BEFORE):
                if n >= 2:
                    emptied(pe, BEFORE[n - 2], -1)
                work((*job, whole_jobs.get(job[0], ())), -1, n % 2).then_inc(job_full, 1)
            score(0, 0)
            macro_tile(0, FIRST)
            with pe.Fori(1, NM - 1) as i:
                macro_tile(i, MIDDLE)
            macro_tile(NM - 1, LAST)
            weighted_values(NM - 1, UNITS - 1)
            done = jobs_before(LAST, NM - 1) + len(LAST.jobs)
            for n, job in enumerate(AFTER):
                before = (LAST.jobs + AFTER)[len(LAST.jobs) + n - 2]
                emptied(pe, before, NM if before in AFTER and n >= 2 else NM - 1)
                work((*job, whole_jobs.get(job[0], ())), NM, (done + n) % 2).then_inc(job_full, 1)


def ffn(nc, X, ident, minus_half, w_up, w_gate, w_down, out):
    FC = F // P
    with ExitStack() as ctx:
        def sb(name, shape, dt=F32):
            return ctx.enter_context(nc.sbuf_tensor(name, shape, dt))

        ternary = [sb("up_q", [P, DC, F], F16), sb("gate_q", [P, DC, F], F16), sb("down_q", [P, FC, D], F16)]
        up_q, gate_q, down_q = ternary
        w_mean = sb("w_mean", [P, 3])
        sig_scale = sb("sig_scale", [P, 1])
        y_scale = sb("y_scale", [P, 1])
        y_scale_sq = sb("y_scale_sq", [P, 1])
        quantise(nc, ternary, w_mean, sig_scale, y_scale, y_scale_sq, (w_up, w_gate, w_down))

        xn = sb("fxn", [P, TT, D])
        xT_hi = sb("xT_hi", [P, DC, MT], F16)
        xT_lo = sb("xT_lo", [P, DC, MT], F16)
        sig = sb("sig", [P, 2, MT])
        su = sb("su", [P, 2, MT])
        hid = sb("hid", [P, 2, MT])
        h_hi = sb("h_hi", [P, 2, MT], F16)
        h_lo = sb("h_lo", [P, 2, MT], F16)
        y_sb = sb("fy_sb", [P, TT, D])
        z_sb = sb("fz_sb", [P, TT, D])
        o_sb = sb("o_sb", [P, TT, D])
        st_x, mv_x = sb("fst_x", [P, TT, 6]), sb("fmv_x", [P, TT, 2])
        st_y, mv_y = sb("fst_y", [P, TT, 6]), sb("fmv_y", [P, TT, 2])
        var_x, rstd_x = sb("fvar_x", [P, TT]), sb("frstd_x", [P, TT])
        var_y, pow_y, rstd_y = sb("fvar_y", [P, TT]), sb("fpow_y", [P, TT]), sb("frstd_y", [P, TT])

        def ps(name):
            return ctx.enter_context(nc.psum_tensor(name, [P, 512], F32))

        def sem(name):
            return ctx.enter_context(nc.semaphore(name))

        U_ps, G_ps = [ps("U0"), ps("U1")], [ps("G0"), ps("G1")]
        Y_ps = [ps(f"Y{t}") for t in range(TT)]

        up_done, gate_done, sig_done, su_done, hid_done = (
            sem("up_done"), sem("gate_done"), sem("sig_done"), sem("su_done"), sem("hid_done"))
        h_hi_done, h_lo_done, down_done = sem("h_hi_done"), sem("h_lo_done"), sem("down_done")
        xt_done, xT_hi_done, xT_lo_done = sem("xt_done"), sem("xT_hi_done"), sem("xT_lo_done")
        x_stats, x_mv, x_var, x_rstd, xn_done = (
            sem("fx_stats"), sem("fx_mv"), sem("fx_var"), sem("fx_rstd"), sem("fxn_done"))
        y_copied, y_stats, y_mv, y_var, y_pow, y_rstd, z_done, o_done = (
            sem("fy_copied"), sem("fy_stats"), sem("fy_mv"), sem("fy_var"), sem("fy_pow"), sem("fy_rstd"),
            sem("fz_done"), sem("o_done"))
        stored = sem("stored")

        T_ps = [U_ps[0], G_ps[0], U_ps[1], G_ps[1]]
        block = ctx.enter_context(nc.Block())

        @block.sync
        def _(sp):
            out_tiles = out.rearrange("b (n p) d -> p (b n) d", p=P)

            def store(m):
                finished, at = worked_out(sp, TT * (m + 1), m * TT)
                sp.wait_ge(o_done, finished)
                sp.dma_start(out_tiles[:, bass.ds(at, TT), :], o_sb[:]).then_inc(stored, 16)

            store(0)
            with sp.Fori(1, NM) as m:
                store(m)
            sp.wait_ge(stored, 16 * NM)

        @block.gpsimd
        def _(pool):
            def rstd_of_x(m):
                moments = worked_out(pool, TT * (m + 1))[0]
                settled(pool, x_mv)
                pool.wait_ge(x_mv, moments)
                pool.tensor_scalar(var_x[:], mv_x[:, :, 1], EPS, None, ALU.add).then_inc(x_var, 1)
                pool.wait_ge(x_var, m + 1)
                pool.tensor_tensor(rstd_x[:], var_x[:], minus_half[:], ALU.pow).then_inc(x_rstd, 1)

            def finish(m):
                moments, uses = worked_out(pool, TT * (m + 1), m + 1)
                settled(pool, x_mv)
                pool.wait_ge(y_mv, moments)
                pool.tensor_scalar(var_y[:], mv_y[:, :, 1], y_scale_sq[:], EPS, ALU.mult, ALU.add).then_inc(y_var, 1)
                pool.wait_ge(y_var, m + 1)
                pool.tensor_tensor(pow_y[:], var_y[:], minus_half[:], ALU.pow).then_inc(y_pow, 1)
                settled(pool, x_mv)
                pool.wait_ge(y_pow, uses)
                pool.tensor_scalar(rstd_y[:], pow_y[:], y_scale[:], None, ALU.mult).then_inc(y_rstd, 1)
                at_least(pool, stored, 16 * m)
                for t in range(TT):
                    pool.wait_ge(z_done, TT * m + t + 1)
                    pool.tensor_tensor(o_sb[:, t:t + 1, :], X[:, bass.ds(m * TT + t, 1), :], z_sb[:, t:t + 1, :],
                                       ALU.add).then_inc(o_done, 1)

            rstd_of_x(0)
            rstd_of_x(1)
            with pool.Fori(0, NM - 2) as m:
                finish(m)
                rstd_of_x(m + 2)
            finish(NM - 2)
            finish(NM - 1)

        @block.scalar
        def _(act):
            def sigmoid(m, c):
                act.wait_ge(up_done, m * FC + c + 1)
                at_least(act, su_done, m * FC + c - 1)
                nc.scalar.activation(sig[:, c % 2, :], U_ps[c % 2][:], ACT.Sigmoid,
                                     scale=sig_scale[:]).then_inc(sig_done, 1)

            def transposed(m):
                for k in range(DC):
                    act.wait_ge(xt_done, m * DC + k + 1)
                    nc.scalar.activation(xT_hi[:, k, :], T_ps[k][:], ACT.Copy, scale=XN_SCALE).then_inc(xT_hi_done, 1)

            def high(m, c):
                act.wait_ge(hid_done, m * FC + c + 1)
                at_least(act, down_done, m * FC + c - 1)
                nc.scalar.activation(h_hi[:, c % 2, :], hid[:, c % 2, :], ACT.Copy).then_inc(h_hi_done, 1)

            def macro_tile(m, last):
                for c in range(FC):
                    if c + 1 < FC:
                        sigmoid(m, c + 1)
                    elif not last:
                        transposed(m + 1)
                    high(m, c)
                if not last:
                    sigmoid(m + 1, 0)
                for t in range(TT):
                    act.wait_ge(down_done, (m + 1) * FC)
                    at_least(act, z_done, (m - 1) * TT + t + 1)
                    nc.scalar.activation(y_sb[:, t, :], Y_ps[t][:], ACT.Copy).then_inc(y_copied, 1)

            transposed(0)
            sigmoid(0, 0)
            macro_tile(0, False)
            with act.Fori(1, NM - 1) as m:
                macro_tile(m, False)
            macro_tile(NM - 1, True)

        @block.vector
        def _(dve):
            def statistics(m):
                for t in range(TT):
                    nc.vector.bn_stats(st_x[:, t, :], X[:, bass.ds(m * TT + t, 1), :]).then_inc(x_stats, 1)
                counts = worked_out(dve, *(m * TT + t + 1 for t in range(TT)))
                for t in range(TT):
                    settled(dve, x_stats)
                    dve.wait_ge(x_stats, counts[t])
                    nc.vector.bn_aggr(mv_x[:, t, :], st_x[:, t, :]).then_inc(x_mv, 1)

            def layer_norm(m, t):
                dve.wait_ge(x_rstd, m + 1)
                nc.vector.tensor_scalar(xn[:, t:t + 1, :], X[:, bass.ds(m * TT + t, 1), :], mv_x[:, t, 0:1],
                                        rstd_x[:, t:t + 1], ALU.subtract, ALU.mult).then_inc(xn_done, 1)

            def transposed(m):
                for k in range(DC):
                    dve.wait_ge(xT_hi_done, m * DC + k + 1)
                    nc.vector.scalar_tensor_tensor(xT_lo[:, k, :], T_ps[k][:], XN_SCALE, xT_hi[:, k, :],
                                                   ALU.mult, ALU.subtract).then_inc(xT_lo_done, 1)

            def hidden(m, c):
                n = m * FC + c
                dve.wait_ge(sig_done, n + 1)
                nc.vector.scalar_tensor_tensor(su[:, c % 2, :], U_ps[c % 2][:], H_SCALE / XN_SCALE ** 2, sig[:, c % 2, :],
                                               ALU.mult, ALU.mult).then_inc(su_done, 1)
                dve.wait_ge(su_done, n + 1)
                dve.wait_ge(gate_done, n + 1)
                at_least(dve, h_hi_done, n - 1)
                nc.vector.tensor_tensor(hid[:, c % 2, :], G_ps[c % 2][:], su[:, c % 2, :], ALU.mult).then_inc(hid_done, 1)

            def low(m, c):
                n = m * FC + c
                dve.wait_ge(h_hi_done, n + 1)
                at_least(dve, down_done, n - 1)
                nc.vector.tensor_tensor(h_lo[:, c % 2, :], hid[:, c % 2, :], h_hi[:, c % 2, :],
                                        ALU.subtract).then_inc(h_lo_done, 1)

            def y_statistics(m):
                for t in range(TT):
                    dve.wait_ge(y_copied, m * TT + t + 1)
                    nc.vector.bn_stats(st_y[:, t, :], y_sb[:, t, :]).then_inc(y_stats, 1)
                counts = worked_out(dve, *(m * TT + t + 1 for t in range(TT)))
                for t in range(TT):
                    settled(dve, x_stats)
                    dve.wait_ge(y_stats, counts[t])
                    nc.vector.bn_aggr(mv_y[:, t, :], st_y[:, t, :]).then_inc(y_mv, 1)

            def y_normalise(m, t):
                dve.wait_ge(y_rstd, m + 1)
                nc.vector.tensor_scalar(z_sb[:, t, :], y_sb[:, t, :], mv_y[:, t, 0:1], rstd_y[:, t:t + 1],
                                        ALU.subtract, ALU.mult).then_inc(z_done, 1)

            def macro_tile(m, first, last):
                for c in range(FC):
                    if c + 1 < FC:
                        hidden(m, c + 1)
                    elif not last:
                        transposed(m + 1)
                    low(m, c)
                    if not first:
                        if c == 1:
                            y_statistics(m - 1)
                        if 3 <= c < 3 + TT:
                            y_normalise(m - 1, c - 3)
                    if not last:
                        if c == 7:
                            statistics(m + 1)
                        if 9 <= c < 9 + TT:
                            layer_norm(m + 1, c - 9)
                if not last:
                    hidden(m + 1, 0)

            statistics(0)
            for t in range(TT):
                layer_norm(0, t)
            transposed(0)
            hidden(0, 0)
            macro_tile(0, True, False)
            with dve.Fori(1, NM - 1) as m:
                macro_tile(m, False, False)
            macro_tile(NM - 1, False, True)
            y_statistics(NM - 1)
            for t in range(TT):
                y_normalise(NM - 1, t)

        @block.tensor
        def _(pe):
            def up_gate(m, c):
                n = m * FC + c
                if c >= 2:
                    pe.wait_ge(hid_done, n - 1)
                else:
                    pe.wait_ge(xT_lo_done, DC * (m + 1))
                for w, dst, done in ((up_q, U_ps[c % 2], up_done), (gate_q, G_ps[c % 2], gate_done)):
                    for k in range(DC):
                        for part, xT in enumerate((xT_hi, xT_lo)):
                            e = pe.matmul(dst[:], w[:, k, c * P:(c + 1) * P], xT[:, k, :],
                                          start=(k == 0 and part == 0), stop=(k == DC - 1 and part == 1))
                    e.then_inc(done, 1)

            def down(m, c):
                n = m * FC + c
                pe.wait_ge(h_lo_done, n + 1)
                for t in range(TT):
                    if c == 0:
                        at_least(pe, y_copied, (m - 1) * TT + t + 1)
                    for part, h in enumerate((h_hi, h_lo)):
                        e = pe.matmul(Y_ps[t][:], h[:, c % 2, t * P:(t + 1) * P], down_q[:, c, :],
                                      start=(c == 0 and part == 0), stop=(c == FC - 1 and part == 1))
                e.then_inc(down_done, 1)

            def transposes(m, first):
                pe.wait_ge(xn_done, TT * (m + 1))
                for k in range(DC):
                    if not first:
                        pe.wait_ge(hid_done, m * FC - 1 + k // 2)
                    for t in range(TT):
                        e = pe.transpose(T_ps[k][:, t * P:(t + 1) * P], xn[:, t, k * P:(k + 1) * P], ident[:])
                    e.then_inc(xt_done, 1)

            def macro_tile(m, last):
                for c in range(FC):
                    if c + 1 < FC:
                        up_gate(m, c + 1)
                    elif not last:
                        transposes(m + 1, False)
                    down(m, c)
                if not last:
                    up_gate(m + 1, 0)

            transposes(0, True)
            up_gate(0, 0)
            macro_tile(0, False)
            with pe.Fori(1, NM - 1) as m:
                macro_tile(m, False)
            macro_tile(NM - 1, True)


def quantise(nc, ternary, w_mean, sig_scale, y_scale, y_scale_sq, weights):
    COUNT = D * F
    WIDTH = COUNT // P
    PARTS = 16
    with ExitStack() as ctx:
        def sb(name, shape, dt=F32):
            return ctx.enter_context(nc.sbuf_tensor(name, shape, dt))

        stage = sb("stage", [P, 2, WIDTH])
        below = sb("below", [P, WIDTH], F16)
        ones = sb("ones", [P, P])
        partial = sb("partial", [P, 3, PARTS])
        total = sb("total", [P, 3])
        half, minus_half_mean = sb("half", [P, 3]), sb("minus_half_mean", [P, 3])
        mean_prod = sb("mean_prod", [P, 2])
        sum_ps = ctx.enter_context(nc.psum_tensor("sum_ps", [P, 3, PARTS], F32))
        names = ("w_staged0", "w_staged1", "w_staged2", "ones_set", "partial_done", "summed", "total_done",
                 "mean_done", "thresholds", "below_done", "ternary_done", "prod_done")
        (w0, w1, w2, ones_set, partial_done, summed, total_done, mean_done, thresholds, below_done, ternary_done,
         prod_done) = (ctx.enter_context(nc.semaphore(n)) for n in names)
        staged = (w0, w1, w2)
        block = ctx.enter_context(nc.Block())

        @block.sync
        def _(sp):
            for n, w in enumerate(weights):
                at_least(sp, ternary_done, n - 1)
                sp.dma_start(stage[:, n % 2, :].rearrange("p (c n) -> p c n", n=w.shape[1]),
                             w.rearrange("(c p) n -> p c n", p=P)).then_inc(staged[n], 16)

        @block.tensor
        def _(pe):
            pe.wait_ge(ones_set, 1)
            for n in range(3):
                pe.wait_ge(partial_done, n + 1)
                pe.matmul(sum_ps[:, n, :], ones[:], partial[:, n, :], start=True, stop=True).then_inc(summed, 1)

        @block.vector
        def _(dve):
            nc.vector.memset(ones[:], 1.0).then_inc(ones_set, 1)
            for n in range(3):
                w = stage[:, n % 2, :]
                dve.wait_ge(staged[n], 16)
                nc.vector.tensor_reduce(partial[:, n, :], w.rearrange("p (a b) -> p a b", a=PARTS), AX.X, ALU.add,
                                        apply_absolute_value=True).then_inc(partial_done, 1)
                dve.wait_ge(summed, n + 1)
                nc.vector.tensor_reduce(total[:, n:n + 1], sum_ps[:, n, :], AX.X, ALU.add).then_inc(total_done, 1)
                dve.wait_ge(total_done, n + 1)
                nc.vector.tensor_scalar(w_mean[:, n:n + 1], total[:, n:n + 1], 1.0 / COUNT, 1e-8,
                                        ALU.mult, ALU.add).then_inc(mean_done, 1)
                dve.wait_ge(mean_done, n + 1)
                nc.vector.tensor_scalar(half[:, n:n + 1], w_mean[:, n:n + 1], 0.5, None, ALU.mult).then_inc(thresholds, 1)
                nc.vector.tensor_scalar(minus_half_mean[:, n:n + 1], w_mean[:, n:n + 1], -0.5, None,
                                        ALU.mult).then_inc(thresholds, 1)
                dve.wait_ge(thresholds, 2 * n + 2)
                nc.vector.tensor_scalar(below[:], w, minus_half_mean[:, n:n + 1], None, ALU.is_lt).then_inc(below_done, 1)
                dve.wait_ge(below_done, n + 1)
                flat = ternary[n][:].rearrange("p c n -> p (c n)")
                nc.vector.scalar_tensor_tensor(flat, w, half[:, n:n + 1], below[:],
                                               ALU.is_gt, ALU.subtract).then_inc(ternary_done, 1)
            nc.vector.tensor_scalar(sig_scale[:], w_mean[:, 0:1], 1.0 / XN_SCALE, None, ALU.mult).then_inc(prod_done, 1)
            nc.vector.tensor_tensor(mean_prod[:, 0:1], w_mean[:, 0:1], w_mean[:, 1:2], ALU.mult).then_inc(prod_done, 1)
            dve.wait_ge(prod_done, 2)
            nc.vector.tensor_tensor(mean_prod[:, 1:2], mean_prod[:, 0:1], w_mean[:, 2:3], ALU.mult).then_inc(prod_done, 1)
            dve.wait_ge(prod_done, 3)
            nc.vector.tensor_scalar(y_scale[:], mean_prod[:, 1:2], 1.0 / H_SCALE, None, ALU.mult).then_inc(prod_done, 1)
            dve.wait_ge(prod_done, 4)
            nc.vector.tensor_tensor(y_scale_sq[:], y_scale[:], y_scale[:], ALU.mult).then_inc(prod_done, 1)


def rope_tables():
    inv_freq = np.float32(1.0) / np.power(np.float32(10000.0), np.arange(0, HD, 2, dtype=np.float32) / np.float32(HD))
    angle = (np.arange(SEQ, dtype=np.float32)[:, None] * inv_freq[None, :]).astype(np.float64)
    sign = np.where(np.arange(HD) % 2 == 0, -1.0, 1.0)
    cos = np.repeat(np.cos(angle), 2, axis=1)
    sin = np.repeat(np.sin(angle), 2, axis=1) * sign

    def by_tile(t):
        t = np.tile(t.T.astype(np.float32), (P // HD, 1))
        t = t.reshape(P, PER_BATCH, MT).transpose(1, 0, 2)
        return np.ascontiguousarray(np.tile(t, (BATCH, 1, 1)))

    return by_tile(cos), by_tile(sin)


def band_masks():
    q, k = np.arange(P)[:, None], np.arange(2 * P)[None, :]
    seen = (k >= q) & (k <= q + WINDOW)
    masks = np.zeros((NM, P, 2 * P), np.float32)
    for i in range(NM):
        masks[i][~(seen & ((k >= P) | (i % PER_BATCH != 0)))] = NEG
    return masks


def kernel(L0_attn_x, L0_attn_W_qkv, L0_attn_W_out, L0_attn_b_out, L0_ffn_W_up, L0_ffn_W_gate, L0_ffn_W_down):
    import concourse.bacc as bacc
    from concourse.bass_utils import run_bass_kernel_spmd

    cos_t, sin_t = rope_tables()
    arrays = {
        "x": np.ascontiguousarray(L0_attn_x),
        "w_qkv": np.ascontiguousarray(np.asarray(L0_attn_W_qkv).reshape(D, D, 3).transpose(2, 0, 1)),
        "w_out": np.ascontiguousarray(L0_attn_W_out),
        "b_out": np.ascontiguousarray(L0_attn_b_out),
        "w_up": np.ascontiguousarray(np.asarray(L0_ffn_W_up).T),
        "w_gate": np.ascontiguousarray(np.asarray(L0_ffn_W_gate).T),
        "w_down": np.ascontiguousarray(np.asarray(L0_ffn_W_down).T),
        "cos_t": cos_t,
        "sin_t": sin_t,
        "bands": band_masks(),
        "ident": np.eye(P, dtype=np.float32),
    }
    nc = bacc.Bacc("TRN2", target_bir_lowering=False, num_devices=1)
    ins = [nc.dram_tensor(f"in_{k}", a.shape, mybir.dt.from_np(a.dtype), kind="ExternalInput").ap()
           for k, a in arrays.items()]
    out = nc.dram_tensor("out_x", (BATCH, SEQ, D), F32, kind="ExternalOutput").ap()
    layer(nc, *ins, out)
    r = run_bass_kernel_spmd(nc, [{f"in_{k}": a for k, a in arrays.items()}], core_ids=[0])
    return r.results[0]["out_x"]
```

```python
from contextlib import ExitStack

import numpy as np

import concourse.bass as bass
from concourse import mybir

P = 128
F32 = mybir.dt.float32
F16 = mybir.dt.float16
I32 = mybir.dt.int32
ALU = mybir.AluOpType
ACT = mybir.ActivationFunctionType
AX = mybir.AxisListType

D = 512
H = 16
HD = D // H
WINDOW = P
F = 2048
BATCH, SEQ = 2, 2048
TOK = BATCH * SEQ
MT = 512
NM = TOK // MT
TT = MT // P
DC = D // P
NG = H // 4
STEPS = TT * 2
UNITS = NG * STEPS
PER_BATCH = SEQ // MT
EPS = 1e-5

QKV_SCALE = 32.0
P_SCALE = 2.0 ** 14
XN_SCALE = 2.0 ** 10
H_SCALE = 2.0 ** -3
PARTS = 16
NEG = -1.0e38


FILLER = [
    [("V", 1, (0, 1))],
    [("V", 1, (2, 3))],
    [("OT", 3, ()), ("VT", 1, ())],
    [("Y", 0, (0, 1))],
    [("Y", 0, (2, 3)), ("Q", 2, (0,))],
    [("Q", 2, (1, 2, 3))],
    [("K", 2, (0, 1))],
    [("K", 2, (2, 3))],
    [("V", 2, (0, 1))],
    [("V", 2, (2, 3))],
    [("VT", 2, ()), ("Y", 1, (0,))],
    [("Y", 1, (1, 2))],
    [("Y", 1, (3,)), ("Q", 3, (0,))],
    [("Q", 3, (1, 2, 3))],
    [("K", 3, (0, 1))],
    [("K", 3, (2, 3))],
    [("V", 3, (0, 1, 2))],
    [("V", 3, (3,)), ("Y", 2, (0, 1))],
    [("Y", 2, (2, 3)), ("VT", 3, ())],
    [("T", 0, ()), ("T", 1, ())],
    [("T", 2, ()), ("T", 3, ())],
    [("Q", 0, (0, 1, 2))],
    [("Q", 0, (3,)), ("K", 0, (0,))],
    [("K", 0, (1, 2, 3))],
    [("V", 0, (0, 1, 2))],
    [("V", 0, (3,)), ("Y", 3, (0, 1))],
    [("Y", 3, (2, 3)), ("VT", 0, ())],
    [("OT", 0, ()), ("OT", 1, ())],
    [("OT", 2, ()), ("Q", 1, (0, 1))],
    [("Q", 1, (2, 3))],
    [("K", 1, (0, 1))],
    [("K", 1, (2, 3))],
]
BEFORE = ([("T", k) for k in range(DC)]
          + [("Q", 0), ("K", 0), ("V", 0), ("VT", 0), ("Q", 1), ("K", 1)])
AFTER = [("OT", 3)] + [("Y", t) for t in range(TT)]


def is_ahead(job):
    kind, idx = job
    return kind == "T" or kind in ("V", "VT") and idx == 0 or kind in ("Q", "K") and idx <= 1


def is_behind(job):
    return job[0] == "Y" or job == ("OT", 3)


class Plan:

    def __init__(self, of_previous, of_next):
        def kept(job):
            if is_behind(job):
                return of_previous
            return of_next or not is_ahead(job)

        self.steps = [[p for p in step if kept(p[:2])] for step in FILLER]
        self.jobs = []
        self.ends = [[] for _ in self.steps]
        for step in self.steps:
            for kind, idx, _ in step:
                if (kind, idx) not in self.jobs:
                    self.jobs.append((kind, idx))
        for job in self.jobs:
            self.ends[max(s for s, step in enumerate(self.steps) for p in step if p[:2] == job)].append(job)
        assert self.jobs == [job for jobs in self.ends for job in jobs]


FIRST, MIDDLE, LAST = Plan(False, True), Plan(True, True), Plan(True, False)
assert len(MIDDLE.jobs) % 2 == 0 and FIRST.jobs[-2:] == MIDDLE.jobs[-2:]


def jobs_before(plan, i):
    if plan is FIRST:
        return len(BEFORE)
    return len(BEFORE) + len(FIRST.jobs) - len(MIDDLE.jobs) + i * len(MIDDLE.jobs)


def bank_of(plan, n):
    return (len(BEFORE) + (0 if plan is FIRST else len(FIRST.jobs)) + n) % 2


def tile_of(job, i):
    return i - 1 if is_behind(job) else i + 1 if is_ahead(job) else i


def at_least(engine, semaphore, value):
    if isinstance(value, int) and value <= 0:
        return
    engine.wait_ge(semaphore, value)


def worked_out(engine, *values):
    return [v if isinstance(v, int) else engine.snap(engine.to_reg(v)) for v in values]


def settled(engine, semaphore):
    engine.wait_ge(semaphore, 1)


def layer(nc, x, w_qkv, w_out, b_out, w_up, w_gate, w_down, cos_t, sin_t, bands, ident_in, out):
    with ExitStack() as whole:
        X = whole.enter_context(nc.sbuf_tensor("X", [P, NM * TT, D], F32))
        ident = whole.enter_context(nc.sbuf_tensor("ident", [P, P], F32))
        minus_half = whole.enter_context(nc.sbuf_tensor("minus_half", [P, TT], F32))
        weights = whole.enter_context(nc.sbuf_tensor("weights", [P, D * F // P], F32))
        w_up_in = whole.enter_context(nc.semaphore("w_up_in"))
        partial = whole.enter_context(nc.sbuf_tensor("partial", [P, 3, PARTS], F32))
        attention(nc, X, ident, minus_half, weights, w_up_in, w_up, partial,
                  x, w_qkv, w_out, b_out, cos_t, sin_t, bands, ident_in)
        ffn(nc, X, ident, minus_half, weights, partial, w_gate, w_down, out)


def attention(nc, X, ident, minus_half, weights, w_up_in, w_up, partial,
              x, w_qkv, w_out, b_out, cos_t, sin_t, bands, ident_in):
    with ExitStack() as ctx:
        def sb(name, shape, dt=F32):
            return ctx.enter_context(nc.sbuf_tensor(name, shape, dt))

        def ps(name):
            return ctx.enter_context(nc.psum_tensor(name, [P, 512], F32))

        def sem(name):
            return ctx.enter_context(nc.semaphore(name))

        W = weights[:, 0:3 * DC * D].rearrange("p (s c n) -> p s c n", s=3, c=DC)
        Wo = sb("Wo", [P, DC, D])
        bias_bc = sb("bias_bc", [P, D])
        cosT = sb("cosT", [P, MT])
        sinT = sb("sinT", [P, MT])
        band = sb("band", [P, 2 * P])
        band0 = sb("band0", [P, 2 * P])
        xn = sb("xn", [P, TT, D])
        xnT = sb("xnT", [P, DC, MT])
        st_x = sb("st_x", [P, TT, 6])
        mv_x = sb("mv_x", [P, TT, 2])
        var_x = sb("var_x", [P, TT])
        rstd_x = sb("rstd_x", [P, TT])
        st_y = sb("st_y", [P, TT, 6])
        mv_y = sb("mv_y", [P, TT, 2])
        var_y = sb("var_y", [P, TT])
        rstd_y = sb("rstd_y", [P, TT])
        rot = sb("rot", [P, 2, MT])
        swp = sb("swp", [P, 2, MT])
        split = sb("split", [P, 2, 2, MT], F16)
        Qp = sb("Qp", [P, 2, 4, MT], F16)
        Kp = sb("Kp", [P, 2, 4, MT], F16)
        Kc = sb("Kc", [P, H, P], F16)
        vT = sb("vT", [P, MT])
        Vp = sb("Vp", [P, 2, TT, 4, 2 * HD], F16)
        Vc = sb("Vc", [P, H, 2 * HD], F16)
        prob = sb("prob", [P, 4, 2, 2 * P])
        peak = sb("peak", [P, 4, 2])
        rsum = sb("rsum", [P, 2, 4])
        rinv = sb("rinv", [P, 2, 4])
        p_hi = sb("p_hi", [P, 2, 4, P], F16)
        p_lo = sb("p_lo", [P, 2, 4, P], F16)
        o_raw = sb("o_raw", [P, 2, 4, HD])
        o_n = sb("o_n", [P, NG, TT, 4, HD])
        oT = sb("oT", [P, NG, MT])
        y_sb = sb("y_sb", [P, TT, D])
        wmax, wmax_all, p2, p2_inv, p2_sq = (sb(n, [P, 1]) for n in ("wmax", "wmax_all", "p2", "p2_inv", "p2_sq"))
        wmax_parts = sb("wmax_parts", [P, 3])
        p2_bits = sb("p2_bits", [P, 1], I32)
        w_scale, neg_score_scale, o_scale = (sb(n, [P, 1]) for n in ("w_scale", "neg_score_scale", "o_scale"))

        spill = nc.dram_tensor("spill", [2, 2, P, MT], F16).ap()

        S_ps = [ps("S0"), ps("S1")]
        PT_ps = [ps("PT0"), ps("PT1")]
        O_ps = [ps("O0"), ps("O1")]
        J_ps = [ps("J0"), ps("J1")]

        x0_in, x1_in, x_rest_in, wo_in = sem("x0_in"), sem("x1_in"), sem("x_rest_in"), sem("wo_in")
        w_in = [sem(f"w_{part}_in") for part in "qkv"]
        const_in, bias_in, table_in, band0_in = sem("const_in"), sem("bias_in"), sem("table_in"), sem("band0_in")
        q_spilled, k_spilled, q_packed, k_packed = sem("q_spilled"), sem("k_spilled"), sem("q_packed"), sem("k_packed")
        set_up, wmax_parts_done, wmax_done, wmax_spread, scales = (
            sem("set_up"), sem("wmax_parts_done"), sem("wmax_done"), sem("wmax_spread"), sem("scales"))
        score_done, logit_done, exp_done, pt_done = sem("score_done"), sem("logit_done"), sem("exp_done"), sem("pt_done")
        p_hi_done, p_lo_done, av_done = sem("p_hi_done"), sem("p_lo_done"), sem("av_done")
        o_read, o_inv, o_norm = sem("o_read"), sem("o_inv"), sem("o_norm")
        job_full = sem("job_full")
        cos_done, swap_done, vT_done, v_hi_done, v_lo_done = (
            sem("cos_done"), sem("swap_done"), sem("vT_done"), sem("v_hi_done"), sem("v_lo_done"))
        xnT_done, oT_done, y_copied = sem("xnT_done"), sem("oT_done"), sem("y_copied")
        sin_done, rot_done, r_hi_done, r_lo_done = sem("sin_done"), sem("rot_done"), sem("r_hi_done"), sem("r_lo_done")
        k_carried, v_carried = sem("k_carried"), sem("v_carried")
        x_stats, x_mv, x_var, x_rstd, xn_done = sem("x_stats"), sem("x_mv"), sem("x_var"), sem("x_rstd"), sem("xn_done")
        y_stats, y_mv, y_var, y_rstd = sem("y_stats"), sem("y_mv"), sem("y_var"), sem("y_rstd")
        z_done, x1_done = sem("z_done"), sem("x1_done")

        def emptied(engine, job, i):
            kind, idx = job
            i = tile_of(job, i)
            if kind in ("Q", "K"):
                at_least(engine, swap_done, 2 * (i * NG + idx) + (1 if kind == "Q" else 2))
            elif kind == "V":
                at_least(engine, vT_done, i * NG + idx + 1)
            elif kind == "VT":
                at_least(engine, v_lo_done, i * NG + idx + 1)
            elif kind == "OT":
                at_least(engine, oT_done, i * NG + idx + 1)
            elif kind == "T":
                at_least(engine, xnT_done, i * DC + idx + 1)
            elif kind == "Y":
                at_least(engine, y_copied, i * TT + idx + 1)

        block = ctx.enter_context(nc.Block())

        @block.sync
        def _(sp):
            x_tiles = x.rearrange("b (n p) d -> p (b n) d", p=P)
            sp.dma_start(X[:, 0:TT, :], x_tiles[:, 0:TT, :]).then_inc(x0_in, 16)
            sp.dma_start(ident[:], ident_in).then_inc(const_in, 16)
            for part in range(3):
                sp.dma_start(W[:, part], w_qkv[part].rearrange("(c p) n -> p c n", p=P)).then_inc(w_in[part], 16)
            sp.dma_start(band[:], bands[1]).then_inc(const_in, 16)
            sp.dma_start(cosT[:], cos_t[0]).then_inc(table_in, 16)
            sp.dma_start(sinT[:], sin_t[0]).then_inc(table_in, 16)
            sp.dma_start(band0[:], bands[0]).then_inc(band0_in, 16)
            sp.dma_start(X[:, TT:2 * TT, :], x_tiles[:, TT:2 * TT, :]).then_inc(x1_in, 16)
            sp.dma_start(Wo[:], w_out.rearrange("(c p) n -> p c n", p=P)).then_inc(wo_in, 16)
            sp.dma_start(bias_bc[:], b_out.rearrange("(a n) -> a n", a=1).to_broadcast([P, D])).then_inc(bias_in, 16)
            sp.dma_start(X[:, 2 * TT:, :], x_tiles[:, 2 * TT:, :]).then_inc(x_rest_in, 16)

            def pack(i, g):
                n = i * NG + g
                q_split, k_split, packed_before, written, scored, carried = worked_out(
                    sp, 2 * n + 1, 2 * n + 2, 64 * n, 16 * (n + 1), (n - 1) * STEPS, n - 1)
                sp.wait_ge(r_lo_done, q_split)
                at_least(sp, q_packed, packed_before)
                sp.dma_start(spill[0].rearrange("s p t -> p s t"), split[:, 0]).then_inc(q_spilled, 16)
                sp.wait_ge(q_spilled, written)
                at_least(sp, score_done, scored)
                for row, part in enumerate((0, 0, 1, 1)):
                    sp.dma_start(Qp[row * HD:(row + 1) * HD, g % 2],
                                 spill[0, part].rearrange("(h d) t -> d h t", h=4)).then_inc(q_packed, 16)
                sp.wait_ge(r_lo_done, k_split)
                at_least(sp, k_packed, packed_before)
                sp.dma_start(spill[1].rearrange("s p t -> p s t"), split[:, 1]).then_inc(k_spilled, 16)
                sp.wait_ge(k_spilled, written)
                at_least(sp, k_carried, carried)
                for row, part in enumerate((0, 1, 0, 1)):
                    sp.dma_start(Kp[row * HD:(row + 1) * HD, g % 2],
                                 spill[1, part].rearrange("(h d) t -> d h t", h=4)).then_inc(k_packed, 16)

            def macro_tile(i, plan):
                pack(i, 2)
                pack(i, 3)
                if plan is LAST:
                    sp.wait_ge(job_full, jobs_before(plan, i) + plan.jobs.index(("V", 3)) + 1)
                    sp.dma_start(weights[:].rearrange("p (c n) -> p c n", n=F),
                                 w_up.rearrange("(c p) n -> p c n", p=P)).then_inc(w_up_in, 16)
                    return
                rotations, next_tile = worked_out(sp, 2 * NG * (i + 1), i + 1)
                used = worked_out(sp, i * UNITS + (NG - 1) * STEPS + 2)[0]
                sp.wait_ge(cos_done, rotations)
                sp.wait_ge(sin_done, rotations)
                sp.dma_start(cosT[:], row(cos_t, next_tile)).then_inc(table_in, 16)
                sp.dma_start(sinT[:], row(sin_t, next_tile)).then_inc(table_in, 16)
                pack(i + 1, 0)
                sp.wait_ge(logit_done, used)
                sp.dma_start(band0[:], row(bands, next_tile)).then_inc(band0_in, 16)
                pack(i + 1, 1)

            def row(t, n):
                return t[bass.ds(n, 1)].rearrange("a p k -> (a p) k")

            pack(0, 0)
            pack(0, 1)
            macro_tile(0, FIRST)
            with sp.Fori(1, NM - 1) as i:
                macro_tile(i, MIDDLE)
            macro_tile(NM - 1, LAST)

        @block.gpsimd
        def _(pool):
            pool.memset(minus_half[:], -0.5).then_inc(set_up, 1)
            pool.memset(Kc[:], 0.0).then_inc(set_up, 1)
            pool.memset(Vc[:], 0.0).then_inc(set_up, 1)
            pool.wait_ge(set_up, 3)

            def rstd_of_x(i):
                moments = worked_out(pool, TT * (i + 1))[0]
                settled(pool, set_up)
                pool.wait_ge(x_mv, moments)
                pool.tensor_scalar(var_x[:], mv_x[:, :, 1], EPS, None, ALU.add).then_inc(x_var, 1)
                pool.wait_ge(x_var, i + 1)
                pool.tensor_tensor(rstd_x[:], var_x[:], minus_half[:], ALU.pow).then_inc(x_rstd, 1)

            def rstd_of_y(i, t):
                n = i * TT + t + 1
                moments = worked_out(pool, n)[0]
                settled(pool, set_up)
                pool.wait_ge(y_mv, moments)
                pool.tensor_scalar(var_y[:, t:t + 1], mv_y[:, t, 1:2], EPS, None, ALU.add).then_inc(y_var, 1)
                pool.wait_ge(y_var, n)
                pool.tensor_tensor(rstd_y[:, t:t + 1], var_y[:, t:t + 1], minus_half[:, t:t + 1],
                                   ALU.pow).then_inc(y_rstd, 1)

            def rotate(i, g):
                n = 2 * (i * NG + g)

                def times_sin(a):
                    pool.wait_ge(swap_done, n + a + 1)
                    pool.tensor_tensor(swp[:, a, :], swp[:, a, :], sinT[:], ALU.mult).then_inc(sin_done, 1)

                def add(a):
                    pool.wait_ge(cos_done, n + a + 1)
                    pool.wait_ge(sin_done, n + a + 1)
                    pool.tensor_tensor(rot[:, a, :], rot[:, a, :], swp[:, a, :], ALU.add).then_inc(rot_done, 1)

                def low(a):
                    pool.wait_ge(r_hi_done, n + a + 1)
                    pool.tensor_tensor(split[:, a, 1], rot[:, a, :], split[:, a, 0], ALU.subtract).then_inc(r_lo_done, 1)

                times_sin(0)
                add(0)
                times_sin(1)
                low(0)
                add(1)
                low(1)

            def residual(i, t):
                pool.wait_ge(z_done, TT * i + t + 1)
                row = X[:, bass.ds(i * TT + t, 1), :]
                pool.tensor_tensor(row, row, y_sb[:, t:t + 1, :], ALU.add).then_inc(x1_done, 1)

            def macro_tile(i, plan):
                for g in range(NG):
                    if plan is not LAST and g == 1:
                        rstd_of_x(i + 1)
                    if plan is not FIRST:
                        rstd_of_y(i - 1, g)
                    if g < 2:
                        rotate(i, g + 2)
                    elif plan is not LAST:
                        rotate(i + 1, g - 2)
                    if plan is not FIRST:
                        residual(i - 1, g)

            rstd_of_x(0)
            pool.wait_ge(wmax_done, 1)
            pool.partition_all_reduce(wmax_all[:], wmax[:], P, bass.bass_isa.ReduceOp.max).then_inc(wmax_spread, 1)
            rotate(0, 0)
            rotate(0, 1)
            macro_tile(0, FIRST)
            with pool.Fori(1, NM - 1) as i:
                macro_tile(i, MIDDLE)
            macro_tile(NM - 1, LAST)
            for t in range(TT):
                rstd_of_y(NM - 1, t)
            for t in range(TT):
                residual(NM - 1, t)

        @block.scalar
        def _(act):
            def empty(job, i, number, bank):
                kind, g = job
                n = tile_of(job, i) * NG + g
                if kind == "V":
                    act.wait_ge(job_full, number + 1)
                    nc.scalar.activation(vT[:], J_ps[bank][:], ACT.Copy).then_inc(vT_done, 1)
                elif kind == "VT":
                    act.wait_ge(job_full, number + 1)
                    at_least(act, av_done, (n - 1) * STEPS)
                    at_least(act, v_carried, n - 1)
                    nc.scalar.activation(Vp[:, g % 2, :, :, 0:HD],
                                         J_ps[bank][:].rearrange("p (t h d) -> p t h d", t=TT, h=4),
                                         ACT.Copy).then_inc(v_hi_done, 1)
                elif kind == "OT":
                    act.wait_ge(job_full, number + 1)
                    nc.scalar.activation(oT[:, g, :], J_ps[bank][:], ACT.Copy).then_inc(oT_done, 1)
                elif kind == "T":
                    act.wait_ge(job_full, number + 1)
                    nc.scalar.activation(xnT[:, g, :], J_ps[bank][:], ACT.Identity,
                                         scale=w_scale[:]).then_inc(xnT_done, 1)

            def rotated_high(job, i):
                kind, g = job
                a = "QK".index(kind)
                n = tile_of(job, i) * NG + g
                act.wait_ge(rot_done, 2 * n + a + 1)
                at_least(act, (q_spilled, k_spilled)[a], 16 * n)
                nc.scalar.activation(split[:, a, 0], rot[:, a, :], ACT.Copy).then_inc(r_hi_done, 1)

            def exp(i, u):
                act.wait_ge(logit_done, i * UNITS + u + 1)
                if u % 2 == 0:
                    at_least(act, o_inv, i * (UNITS // 2) + u // 2 - 1)
                for h in range(2):
                    col = 2 * (u % 2) + h
                    e = nc.scalar.activation(prob[:, u % 4, h, :], prob[:, u % 4, h, :], ACT.Exp,
                                             bias=peak[:, u % 4, h:h + 1], scale=-1.0,
                                             accum_out=rsum[:, u // 2 % 2, col:col + 1])
                e.then_inc(exp_done, 1)

            def p_high(i, u):
                act.wait_ge(pt_done, i * UNITS + u + 1)
                at_least(act, av_done, i * UNITS + u - 1)
                nc.scalar.activation(p_hi[:, u % 2, :, :],
                                     PT_ps[u % 2][:].rearrange("p (a k) -> p a k", a=4),
                                     ACT.Copy, scale=P_SCALE).then_inc(p_hi_done, 1)

            def macro_tile(i, plan):
                for u in range(UNITS):
                    if u + 1 < UNITS or plan is not LAST:
                        exp(i, u + 1)
                    for job in plan.ends[u]:
                        n = plan.jobs.index(job)
                        empty(job, i, jobs_before(plan, i) + n, bank_of(plan, n))
                    p_high(i, u)
                    if u >= 2:
                        rotations = [(job, i) for job in plan.ends[u - 2]]
                    else:
                        rotations = [(job, i - 1) for job in MIDDLE.ends[u - 2]] if plan is not FIRST else []
                    for job, of in rotations:
                        if job[0] in ("Q", "K"):
                            rotated_high(job, of)

            act.wait_ge(scales, 7)
            for n, job in enumerate(BEFORE):
                empty(job, -1, n, n % 2)
                if job == ("V", 0):
                    rotated_high(("Q", 0), -1)
                    rotated_high(("K", 0), -1)
            rotated_high(("Q", 1), -1)
            rotated_high(("K", 1), -1)
            exp(0, 0)
            macro_tile(0, FIRST)
            with act.Fori(1, NM - 1) as i:
                macro_tile(i, MIDDLE)
            macro_tile(NM - 1, LAST)
            done = jobs_before(LAST, NM - 1) + len(LAST.jobs)
            empty(AFTER[0], NM, done, done % 2)
            act.wait_ge(w_up_in, 16)
            part = D * F // P // PARTS
            unused = [t[:].rearrange("p c n -> p (c n)").bitcast(F16) for t in (xn, xnT)]
            for k in range(PARTS):
                at = k // 2 * part
                nc.scalar.activation(unused[k % 2][:, at:at + part], weights[:, k * part:(k + 1) * part], ACT.Abs,
                                     accum_out=partial[:, 0, k:k + 1])

        @block.vector
        def _(dve):
            def layer_norm_stats(i, t):
                x_row = X[:, bass.ds(i * TT + t, 1), :]
                nc.vector.bn_stats(st_x[:, t, :], x_row).then_inc(x_stats, 1)

            def layer_norm_moments(i):
                counts = worked_out(dve, *(i * TT + t + 1 for t in range(TT)))
                for t in range(TT):
                    settled(dve, x0_in)
                    dve.wait_ge(x_stats, counts[t])
                    nc.vector.bn_aggr(mv_x[:, t, :], st_x[:, t, :]).then_inc(x_mv, 1)

            def layer_norm(i, t):
                dve.wait_ge(x_rstd, i + 1)
                x_row = X[:, bass.ds(i * TT + t, 1), :]
                nc.vector.tensor_scalar(xn[:, t:t + 1, :], x_row, mv_x[:, t, 0:1], rstd_x[:, t:t + 1],
                                        ALU.subtract, ALU.mult).then_inc(xn_done, 1)

            def empty(job, i, number, bank):
                kind, g = job
                tile = tile_of(job, i)
                n = tile * NG + g
                if kind in ("Q", "K"):
                    a = 0 if kind == "Q" else 1
                    dve.wait_ge(job_full, number + 1)
                    dve.wait_ge(table_in, 32 * (tile + 1))
                    at_least(dve, r_lo_done, 2 * n + a - 1)
                    nc.vector.tensor_tensor(rot[:, a, :], J_ps[bank][:], cosT[:], ALU.mult).then_inc(cos_done, 1)
                    nc.vector.stream_shuffle(swp[:, a, :], J_ps[bank][:],
                                             [d ^ 1 for d in range(HD)]).then_inc(swap_done, 1)
                elif kind == "VT":
                    dve.wait_ge(v_hi_done, n + 1)
                    nc.vector.tensor_tensor(Vp[:, g % 2, :, :, HD:2 * HD],
                                            J_ps[bank][:].rearrange("p (t h d) -> p t h d", t=TT, h=4),
                                            Vp[:, g % 2, :, :, 0:HD], ALU.subtract).then_inc(v_lo_done, 1)
                elif kind == "Y":
                    dve.wait_ge(job_full, number + 1)
                    nc.vector.tensor_tensor(y_sb[:, g, :], J_ps[bank][:], bias_bc[:], ALU.add).then_inc(y_copied, 1)

            def logits(i, u):
                first_tile = u // 2 % TT == 0
                scored, transposed, bands_in = worked_out(
                    dve, i * UNITS + u + 1, i * UNITS + u - 3, 16 * (i + 1 + u // UNITS))
                settled(dve, x0_in)
                dve.wait_ge(score_done, scored)
                at_least(dve, pt_done, transposed)
                if first_tile and u % 2 == 0:
                    dve.wait_ge(band0_in, bands_in)
                for h in range(2):
                    e = nc.vector.tensor_tensor_reduce(
                        out=prob[:, u % 4, h, :], in0=S_ps[u % 2][:, h * 2 * P:(h + 1) * 2 * P],
                        in1=(band0 if first_tile else band)[:], scale=neg_score_scale[:], scalar=3.0e38,
                        op0=ALU.add, op1=ALU.min, accum_out=peak[:, u % 4, h:h + 1])
                e.then_inc(logit_done, 1)

            def p_low(i, u):
                dve.wait_ge(p_hi_done, i * UNITS + u + 1)
                at_least(dve, av_done, i * UNITS + u - 1)
                nc.vector.scalar_tensor_tensor(p_lo[:, u % 2, :, :],
                                               PT_ps[u % 2][:].rearrange("p (a k) -> p a k", a=4), P_SCALE,
                                               p_hi[:, u % 2, :, :], ALU.mult, ALU.subtract).then_inc(p_lo_done, 1)

            def normalise(i, k, plan=None):
                tile = i * (UNITS // 2) + k
                g, t = k // TT, k % TT
                dve.wait_ge(av_done, 2 * tile + 2)
                nc.vector.tensor_reduce(
                    o_raw[:, k % 2, :, :],
                    O_ps[k % 2][:, 0:4 * 2 * HD].rearrange("p (h s d) -> p h d s", h=4, s=2),
                    AX.X, ALU.add).then_inc(o_read, 1)
                nc.vector.reciprocal(rinv[:, k % 2, :], rsum[:, k % 2, :]).then_inc(o_inv, 1)
                dve.wait_ge(o_read, tile + 1)
                dve.wait_ge(o_inv, tile + 1)
                if t == 0 and plan is not FIRST:
                    before = jobs_before(plan, i)
                    dve.wait_ge(job_full, before + plan.jobs.index(("OT", 3)) + 1 if g == NG - 1 else before)
                nc.vector.scalar_tensor_tensor(
                    o_n[:, g, t, :, :], o_raw[:, k % 2, :, :], o_scale[:],
                    rinv[:, k % 2, :].unsqueeze(2).to_broadcast([P, 4, HD]), ALU.mult, ALU.mult).then_inc(o_norm, 1)

            def carry_k(i, g):
                dve.wait_ge(score_done, (i * NG + g) * STEPS + 2)
                nc.vector.tensor_copy(Kc[:, 4 * g:4 * g + 4, :], Kp[:, g % 2, :, MT - P:MT]).then_inc(k_carried, 1)

            def carry_v(i, g):
                dve.wait_ge(av_done, (i * NG + g) * STEPS + 2)
                nc.vector.tensor_copy(Vc[:, 4 * g:4 * g + 4, :], Vp[:, g % 2, TT - 1, :, :]).then_inc(v_carried, 1)

            def y_statistics(i, t):
                dve.wait_ge(y_copied, i * TT + t + 1)
                nc.vector.bn_stats(st_y[:, t, :], y_sb[:, t, :]).then_inc(y_stats, 1)

            def y_moments(i, t):
                stats = worked_out(dve, i * TT + t + 1)[0]
                settled(dve, x0_in)
                dve.wait_ge(y_stats, stats)
                nc.vector.bn_aggr(mv_y[:, t, :], st_y[:, t, :]).then_inc(y_mv, 1)

            def y_normalise(i, t):
                dve.wait_ge(y_rstd, i * TT + t + 1)
                nc.vector.tensor_scalar(y_sb[:, t, :], y_sb[:, t, :], mv_y[:, t, 0:1], rstd_y[:, t:t + 1],
                                        ALU.subtract, ALU.mult).then_inc(z_done, 1)

            def macro_tile(i, plan):
                for u in range(UNITS):
                    g, s = u // STEPS, u % STEPS
                    if u + 2 < UNITS or plan is not LAST:
                        logits(i, u + 2)
                    for job in plan.ends[u]:
                        n = plan.jobs.index(job)
                        empty(job, i, jobs_before(plan, i) + n, bank_of(plan, n))
                    p_low(i, u)
                    if u % 2 == 0 and u > 0:
                        normalise(i, u // 2 - 1, plan)
                    if u == 0 and plan is not FIRST:
                        normalise(i - 1, UNITS // 2 - 1)
                    if s == 3:
                        carry_k(i, g)
                    if s == 5:
                        carry_v(i, g)
                    if plan is not LAST:
                        if 4 <= u < 4 + TT:
                            if u == 4:
                                dve.wait_ge(x1_in if plan is FIRST else x_rest_in, 16)
                            layer_norm_stats(i + 1, u - 4)
                        if u == 8:
                            layer_norm_moments(i + 1)
                        if 12 <= u < 12 + TT:
                            layer_norm(i + 1, u - 12)
                    for t in range(TT):
                        if ("Y", t) in plan.jobs:
                            end = next(e for e, jobs in enumerate(plan.ends) if ("Y", t) in jobs)
                            if u == end + 1:
                                y_statistics(i - 1, t)
                                y_moments(i - 1, t)
                            if u == end + 3:
                                y_normalise(i - 1, t)

            dve.wait_ge(x0_in, 16)
            for t in range(TT):
                layer_norm_stats(0, t)
            layer_norm_moments(0)
            for t in range(TT):
                layer_norm(0, t)
            for part in range(3):
                dve.wait_ge(w_in[part], 16)
                nc.vector.tensor_reduce(wmax_parts[:, part:part + 1], W[:, part].rearrange("p c n -> p (c n)"), AX.X,
                                        ALU.max, apply_absolute_value=True).then_inc(wmax_parts_done, 1)
            dve.wait_ge(wmax_parts_done, 3)
            nc.vector.tensor_reduce(wmax[:], wmax_parts[:], AX.X, ALU.max).then_inc(wmax_done, 1)
            dve.wait_ge(wmax_spread, 1)
            nc.vector.tensor_scalar(p2_bits[:], wmax_all[:].bitcast(I32), 0x7F800000, None,
                                    ALU.bitwise_and).then_inc(scales, 1)
            dve.wait_ge(scales, 1)
            nc.vector.tensor_scalar(p2[:], p2_bits[:].bitcast(F32), 2.0 ** -33, None, ALU.max).then_inc(scales, 1)
            dve.wait_ge(scales, 2)
            nc.vector.reciprocal(p2_inv[:], p2[:]).then_inc(scales, 1)
            nc.vector.tensor_tensor(p2_sq[:], p2[:], p2[:], ALU.mult).then_inc(scales, 1)
            nc.vector.tensor_scalar(o_scale[:], p2[:], 1.0 / (QKV_SCALE * P_SCALE), None, ALU.mult).then_inc(scales, 1)
            dve.wait_ge(scales, 4)
            nc.vector.tensor_scalar(w_scale[:], p2_inv[:], QKV_SCALE, None, ALU.mult).then_inc(scales, 1)
            nc.vector.tensor_scalar(neg_score_scale[:], p2_sq[:], -float(np.float32(HD ** -0.5)) / QKV_SCALE ** 2,
                                    None, ALU.mult).then_inc(scales, 1)
            dve.wait_ge(scales, 7)
            dve.wait_ge(const_in, 32)
            dve.wait_ge(bias_in, 16)
            dve.wait_ge(set_up, 3)
            for n, job in enumerate(BEFORE):
                empty(job, -1, n, n % 2)
            logits(0, 0)
            logits(0, 1)
            macro_tile(0, FIRST)
            with dve.Fori(1, NM - 1) as i:
                macro_tile(i, MIDDLE)
            macro_tile(NM - 1, LAST)
            i = NM - 1
            normalise(i, UNITS // 2 - 1)
            done = jobs_before(LAST, i) + len(LAST.jobs)
            dve.wait_ge(x1_done, TT * (NM - 1))
            for n, job in enumerate(AFTER):
                empty(job, NM, done + n, (done + n) % 2)
                if job[0] == "Y":
                    y_statistics(i, job[1])
                    y_moments(i, job[1])
            for t in range(TT):
                y_normalise(i, t)

        @block.tensor
        def _(pe):
            def score(i, u):
                g, t, pair = u // STEPS % NG, u // 2 % TT, u % 2
                if u % STEPS == 0:
                    n = i * NG + u // STEPS
                    pe.wait_ge(q_packed, 64 * (n + 1))
                    pe.wait_ge(k_packed, 64 * (n + 1))
                at_least(pe, logit_done, i * UNITS + u - 1)
                for h in range(2):
                    head = 2 * pair + h
                    q = Qp[:, g % 2, head, t * P:(t + 1) * P]
                    at = h * 2 * P
                    if t == 0:
                        pe.matmul(S_ps[u % 2][:, at:at + P], q, Kc[:, 4 * g + head, :], start=True, stop=True)
                        e = pe.matmul(S_ps[u % 2][:, at + P:at + 2 * P], q, Kp[:, g % 2, head, 0:P],
                                      start=True, stop=True)
                    else:
                        e = pe.matmul(S_ps[u % 2][:, at:at + 2 * P], q, Kp[:, g % 2, head, (t - 1) * P:(t + 1) * P],
                                      start=True, stop=True)
                e.then_inc(score_done, 1)

            def transpose_probs(i, u):
                pe.wait_ge(exp_done, i * UNITS + u + 1)
                at_least(pe, p_lo_done, i * UNITS + u - 1)
                for a in range(4):
                    e = pe.transpose(PT_ps[u % 2][:, a * P:(a + 1) * P],
                                     prob[:, u % 4, a // 2, (a % 2) * P:(a % 2 + 1) * P], ident[:])
                e.then_inc(pt_done, 1)

            def weighted_values(i, u):
                g, t, pair = u // STEPS, u // 2 % TT, u % 2
                tile = i * (UNITS // 2) + u // 2
                if u % STEPS == 0:
                    pe.wait_ge(v_lo_done, i * NG + g + 1)
                pe.wait_ge(p_lo_done, i * UNITS + u + 1)
                if pair == 0:
                    at_least(pe, o_read, tile - 1)
                for h in range(2):
                    head = 2 * pair + h
                    dst = O_ps[u // 2 % 2][:, head * 2 * HD:(head + 1) * 2 * HD]
                    for n, (key_tile, part) in enumerate(((0, p_hi), (1, p_hi), (0, p_lo), (1, p_lo))):
                        if t == 0 and key_tile == 0:
                            v = Vc[:, 4 * g + head, :]
                        else:
                            v = Vp[:, g % 2, t - 1 + key_tile, head, :]
                        e = pe.matmul(dst, part[:, u % 2, 2 * h + key_tile, :], v, start=(n == 0), stop=(n == 3))
                e.then_inc(av_done, 1)

            def work(piece, i, bank):
                kind, g, chunks = piece
                i = tile_of((kind, g), i)
                dst = J_ps[bank]
                e = None
                if kind in ("Q", "K", "V"):
                    s = "QKV".index(kind)
                    if 0 in chunks:
                        pe.wait_ge(xnT_done, DC * (i + 1))
                    for c in chunks:
                        e = pe.matmul(dst[:], W[:, s, c, g * P:(g + 1) * P], xnT[:, c, :],
                                      start=(c == 0), stop=(c == DC - 1))
                    return e if DC - 1 in chunks else None
                if kind == "Y":
                    if 0 in chunks:
                        pe.wait_ge(oT_done, NG * (i + 1))
                    for c in chunks:
                        e = pe.matmul(dst[:], oT[:, c, g * P:(g + 1) * P], Wo[:, c, :],
                                      start=(c == 0), stop=(c == NG - 1))
                    return e if NG - 1 in chunks else None
                if kind == "VT":
                    pe.wait_ge(vT_done, i * NG + g + 1)
                    src = [vT[:, t * P:(t + 1) * P] for t in range(TT)]
                elif kind == "OT":
                    pe.wait_ge(o_norm, (i * NG + g + 1) * TT)
                    src = [o_n[:, g, t].rearrange("p h d -> p (h d)") for t in range(TT)]
                else:
                    pe.wait_ge(xn_done, (i + 1) * TT)
                    src = [xn[:, t, g * P:(g + 1) * P] for t in range(TT)]
                for t in range(TT):
                    e = pe.transpose(dst[:, t * P:(t + 1) * P], src[t], ident[:])
                return e

            def fill(piece, i, plan):
                n = plan.jobs.index(piece[:2])
                if 0 in piece[2] or not piece[2]:
                    if n >= 2:
                        emptied(pe, plan.jobs[n - 2], i)
                    elif plan is FIRST:
                        emptied(pe, BEFORE[n - 2], -1)
                    else:
                        emptied(pe, MIDDLE.jobs[n - 2], i - 1)
                e = work(piece, i, bank_of(plan, n))
                if e is not None:
                    e.then_inc(job_full, 1)

            def macro_tile(i, plan):
                for u in range(UNITS):
                    if u + 2 < UNITS or plan is not LAST:
                        score(i, u + 2)
                    for piece in plan.steps[u]:
                        fill(piece, i, plan)
                    transpose_probs(i, u)
                    if u > 0:
                        weighted_values(i, u - 1)
                    elif plan is not FIRST:
                        weighted_values(i - 1, UNITS - 1)

            pe.wait_ge(const_in, 32)
            for part in range(3):
                pe.wait_ge(w_in[part], 16)
            pe.wait_ge(set_up, 3)
            pe.wait_ge(wo_in, 16)
            whole_jobs = {"Q": (0, 1, 2, 3), "K": (0, 1, 2, 3), "V": (0, 1, 2, 3), "Y": (0, 1, 2, 3)}
            for n, job in enumerate(BEFORE):
                if n >= 2:
                    emptied(pe, BEFORE[n - 2], -1)
                work((*job, whole_jobs.get(job[0], ())), -1, n % 2).then_inc(job_full, 1)
            score(0, 0)
            score(0, 1)
            macro_tile(0, FIRST)
            with pe.Fori(1, NM - 1) as i:
                macro_tile(i, MIDDLE)
            macro_tile(NM - 1, LAST)
            weighted_values(NM - 1, UNITS - 1)
            done = jobs_before(LAST, NM - 1) + len(LAST.jobs)
            for n, job in enumerate(AFTER):
                before = (LAST.jobs + AFTER)[len(LAST.jobs) + n - 2]
                emptied(pe, before, NM if before in AFTER and n >= 2 else NM - 1)
                work((*job, whole_jobs.get(job[0], ())), NM, (done + n) % 2).then_inc(job_full, 1)


def ffn(nc, X, ident, minus_half, weights, partial, w_gate, w_down, out):
    FC = F // P
    with ExitStack() as ctx:
        def sb(name, shape, dt=F32):
            return ctx.enter_context(nc.sbuf_tensor(name, shape, dt))

        ternary = [sb("up_q", [P, DC, F], F16), sb("gate_q", [P, DC, F], F16), sb("down_q", [P, FC, D], F16)]
        up_q, gate_q, down_q = ternary
        w_mean = sb("w_mean", [P, 3])
        sig_scale = sb("sig_scale", [P, 1])
        y_scale = sb("y_scale", [P, 1])
        y_scale_sq = sb("y_scale_sq", [P, 1])
        quantise(nc, ternary, w_mean, sig_scale, y_scale, y_scale_sq, weights, partial, (w_gate, w_down))

        xn = sb("fxn", [P, TT, D])
        xT_hi = sb("xT_hi", [P, DC, MT], F16)
        xT_lo = sb("xT_lo", [P, DC, MT], F16)
        sig = sb("sig", [P, 2, MT])
        su = sb("su", [P, 2, MT])
        hid = sb("hid", [P, 2, MT])
        h_hi = sb("h_hi", [P, 2, MT], F16)
        h_lo = sb("h_lo", [P, 2, MT], F16)
        y_sb = sb("fy_sb", [P, TT, D])
        z_sb = sb("fz_sb", [P, TT, D])
        o_sb = sb("o_sb", [P, TT, D])
        st_x, mv_x = sb("fst_x", [P, TT, 6]), sb("fmv_x", [P, TT, 2])
        st_y, mv_y = sb("fst_y", [P, TT, 6]), sb("fmv_y", [P, TT, 2])
        var_x, rstd_x = sb("fvar_x", [P, TT]), sb("frstd_x", [P, TT])
        var_y, pow_y, rstd_y = sb("fvar_y", [P, TT]), sb("fpow_y", [P, TT]), sb("frstd_y", [P, TT])

        def ps(name):
            return ctx.enter_context(nc.psum_tensor(name, [P, 512], F32))

        def sem(name):
            return ctx.enter_context(nc.semaphore(name))

        U_ps, G_ps = [ps("U0"), ps("U1")], [ps("G0"), ps("G1")]
        Y_ps = [ps(f"Y{t}") for t in range(TT)]

        up_done, gate_done, sig_done, su_done, hid_done = (
            sem("up_done"), sem("gate_done"), sem("sig_done"), sem("su_done"), sem("hid_done"))
        h_hi_done, h_lo_done, down_done = sem("h_hi_done"), sem("h_lo_done"), sem("down_done")
        xt_done, xT_hi_done, xT_lo_done = sem("xt_done"), sem("xT_hi_done"), sem("xT_lo_done")
        x_stats, x_mv, x_var, x_rstd, xn_done = (
            sem("fx_stats"), sem("fx_mv"), sem("fx_var"), sem("fx_rstd"), sem("fxn_done"))
        y_copied, y_stats, y_mv, y_var, y_pow, y_rstd, z_done, o_done = (
            sem("fy_copied"), sem("fy_stats"), sem("fy_mv"), sem("fy_var"), sem("fy_pow"), sem("fy_rstd"),
            sem("fz_done"), sem("o_done"))
        stored = sem("stored")

        T_ps = [U_ps[0], G_ps[0], U_ps[1], G_ps[1]]
        block = ctx.enter_context(nc.Block())

        @block.sync
        def _(sp):
            out_tiles = out.rearrange("b (n p) d -> p (b n) d", p=P)

            def store(m):
                finished, at = worked_out(sp, TT * (m + 1), m * TT)
                sp.wait_ge(o_done, finished)
                sp.dma_start(out_tiles[:, bass.ds(at, TT), :], o_sb[:]).then_inc(stored, 16)

            store(0)
            with sp.Fori(1, NM) as m:
                store(m)
            sp.wait_ge(stored, 16 * NM)

        @block.gpsimd
        def _(pool):
            def rstd_of_x(m):
                moments = worked_out(pool, TT * (m + 1))[0]
                settled(pool, x_mv)
                pool.wait_ge(x_mv, moments)
                pool.tensor_scalar(var_x[:], mv_x[:, :, 1], EPS, None, ALU.add).then_inc(x_var, 1)
                pool.wait_ge(x_var, m + 1)
                pool.tensor_tensor(rstd_x[:], var_x[:], minus_half[:], ALU.pow).then_inc(x_rstd, 1)

            def finish(m):
                moments, uses = worked_out(pool, TT * (m + 1), m + 1)
                settled(pool, x_mv)
                pool.wait_ge(y_mv, moments)
                pool.tensor_scalar(var_y[:], mv_y[:, :, 1], y_scale_sq[:], EPS, ALU.mult, ALU.add).then_inc(y_var, 1)
                pool.wait_ge(y_var, m + 1)
                pool.tensor_tensor(pow_y[:], var_y[:], minus_half[:], ALU.pow).then_inc(y_pow, 1)
                settled(pool, x_mv)
                pool.wait_ge(y_pow, uses)
                pool.tensor_scalar(rstd_y[:], pow_y[:], y_scale[:], None, ALU.mult).then_inc(y_rstd, 1)
                at_least(pool, stored, 16 * m)
                for t in range(TT):
                    pool.wait_ge(z_done, TT * m + t + 1)
                    pool.tensor_tensor(o_sb[:, t:t + 1, :], X[:, bass.ds(m * TT + t, 1), :], z_sb[:, t:t + 1, :],
                                       ALU.add).then_inc(o_done, 1)

            rstd_of_x(0)
            rstd_of_x(1)
            with pool.Fori(0, NM - 2) as m:
                finish(m)
                rstd_of_x(m + 2)
            finish(NM - 2)
            finish(NM - 1)

        @block.scalar
        def _(act):
            def sigmoid(m, c):
                act.wait_ge(up_done, m * FC + c + 1)
                at_least(act, su_done, m * FC + c - 1)
                nc.scalar.activation(sig[:, c % 2, :], U_ps[c % 2][:], ACT.Sigmoid,
                                     scale=sig_scale[:]).then_inc(sig_done, 1)

            def transposed(m, chunks=range(DC)):
                for k in chunks:
                    act.wait_ge(xt_done, m * DC + k + 1)
                    nc.scalar.activation(xT_hi[:, k, :], T_ps[k][:], ACT.Copy, scale=XN_SCALE).then_inc(xT_hi_done, 1)

            def high(m, c):
                act.wait_ge(hid_done, m * FC + c + 1)
                at_least(act, down_done, m * FC + c - 1)
                nc.scalar.activation(h_hi[:, c % 2, :], hid[:, c % 2, :], ACT.Copy).then_inc(h_hi_done, 1)

            def macro_tile(m, last):
                for c in range(FC):
                    if c == FC - 1 and not last:
                        transposed(m + 1, (0, 1))
                    high(m, c)
                    if c + 1 < FC:
                        sigmoid(m, c + 1)
                if not last:
                    transposed(m + 1, (2, 3))
                for t in range(TT):
                    act.wait_ge(down_done, (m + 1) * FC)
                    at_least(act, z_done, (m - 1) * TT + t + 1)
                    nc.scalar.activation(y_sb[:, t, :], Y_ps[t][:], ACT.Copy).then_inc(y_copied, 1)
                if not last:
                    sigmoid(m + 1, 0)

            transposed(0)
            sigmoid(0, 0)
            macro_tile(0, False)
            with act.Fori(1, NM - 1) as m:
                macro_tile(m, False)
            macro_tile(NM - 1, True)

        @block.vector
        def _(dve):
            def statistics(m):
                for t in range(TT):
                    nc.vector.bn_stats(st_x[:, t, :], X[:, bass.ds(m * TT + t, 1), :]).then_inc(x_stats, 1)
                counts = worked_out(dve, *(m * TT + t + 1 for t in range(TT)))
                for t in range(TT):
                    settled(dve, x_stats)
                    dve.wait_ge(x_stats, counts[t])
                    nc.vector.bn_aggr(mv_x[:, t, :], st_x[:, t, :]).then_inc(x_mv, 1)

            def layer_norm(m, t):
                dve.wait_ge(x_rstd, m + 1)
                nc.vector.tensor_scalar(xn[:, t:t + 1, :], X[:, bass.ds(m * TT + t, 1), :], mv_x[:, t, 0:1],
                                        rstd_x[:, t:t + 1], ALU.subtract, ALU.mult).then_inc(xn_done, 1)

            def transposed(m, chunks=range(DC)):
                for k in chunks:
                    dve.wait_ge(xT_hi_done, m * DC + k + 1)
                    nc.vector.scalar_tensor_tensor(xT_lo[:, k, :], T_ps[k][:], XN_SCALE, xT_hi[:, k, :],
                                                   ALU.mult, ALU.subtract).then_inc(xT_lo_done, 1)

            def hidden(m, c):
                n = m * FC + c
                dve.wait_ge(sig_done, n + 1)
                nc.vector.scalar_tensor_tensor(su[:, c % 2, :], U_ps[c % 2][:], H_SCALE / XN_SCALE ** 2, sig[:, c % 2, :],
                                               ALU.mult, ALU.mult).then_inc(su_done, 1)
                dve.wait_ge(su_done, n + 1)
                dve.wait_ge(gate_done, n + 1)
                at_least(dve, h_hi_done, n - 1)
                nc.vector.tensor_tensor(hid[:, c % 2, :], G_ps[c % 2][:], su[:, c % 2, :], ALU.mult).then_inc(hid_done, 1)

            def low(m, c):
                n = m * FC + c
                dve.wait_ge(h_hi_done, n + 1)
                at_least(dve, down_done, n - 1)
                nc.vector.tensor_tensor(h_lo[:, c % 2, :], hid[:, c % 2, :], h_hi[:, c % 2, :],
                                        ALU.subtract).then_inc(h_lo_done, 1)

            def y_statistics(m):
                for t in range(TT):
                    dve.wait_ge(y_copied, m * TT + t + 1)
                    nc.vector.bn_stats(st_y[:, t, :], y_sb[:, t, :]).then_inc(y_stats, 1)
                counts = worked_out(dve, *(m * TT + t + 1 for t in range(TT)))
                for t in range(TT):
                    settled(dve, x_stats)
                    dve.wait_ge(y_stats, counts[t])
                    nc.vector.bn_aggr(mv_y[:, t, :], st_y[:, t, :]).then_inc(y_mv, 1)

            def y_normalise(m, t):
                dve.wait_ge(y_rstd, m + 1)
                nc.vector.tensor_scalar(z_sb[:, t, :], y_sb[:, t, :], mv_y[:, t, 0:1], rstd_y[:, t:t + 1],
                                        ALU.subtract, ALU.mult).then_inc(z_done, 1)

            def macro_tile(m, first, last):
                for c in range(FC):
                    if c == FC - 1 and not last:
                        transposed(m + 1, (0, 1))
                    low(m, c)
                    if c + 1 < FC:
                        hidden(m, c + 1)
                    if not first:
                        if c == 1:
                            y_statistics(m - 1)
                        if 3 <= c < 3 + TT:
                            y_normalise(m - 1, c - 3)
                    if not last:
                        if c == 7:
                            statistics(m + 1)
                        if 9 <= c < 9 + TT:
                            layer_norm(m + 1, c - 9)
                if not last:
                    transposed(m + 1, (2, 3))
                    hidden(m + 1, 0)

            statistics(0)
            for t in range(TT):
                layer_norm(0, t)
            transposed(0)
            hidden(0, 0)
            macro_tile(0, True, False)
            with dve.Fori(1, NM - 1) as m:
                macro_tile(m, False, False)
            macro_tile(NM - 1, False, True)
            y_statistics(NM - 1)
            for t in range(TT):
                y_normalise(NM - 1, t)

        @block.tensor
        def _(pe):
            def up_gate(m, c):
                n = m * FC + c
                if c >= 2:
                    pe.wait_ge(hid_done, n - 1)
                for w, dst, done in ((up_q, U_ps[c % 2], up_done), (gate_q, G_ps[c % 2], gate_done)):
                    for k in range(DC):
                        if c == 0:
                            pe.wait_ge(xT_lo_done, DC * m + max(k, 1) + 1)
                        for part, xT in enumerate((xT_hi, xT_lo)):
                            e = pe.matmul(dst[:], w[:, k, c * P:(c + 1) * P], xT[:, k, :],
                                          start=(k == 0 and part == 0), stop=(k == DC - 1 and part == 1))
                    e.then_inc(done, 1)

            def down(m, c):
                n = m * FC + c
                pe.wait_ge(h_lo_done, n + 1)
                for t in range(TT):
                    if c == 0:
                        at_least(pe, y_copied, (m - 1) * TT + t + 1)
                    for part, h in enumerate((h_hi, h_lo)):
                        e = pe.matmul(Y_ps[t][:], h[:, c % 2, t * P:(t + 1) * P], down_q[:, c, :],
                                      start=(c == 0 and part == 0), stop=(c == FC - 1 and part == 1))
                e.then_inc(down_done, 1)

            def transposes(m, first, chunks=range(DC)):
                pe.wait_ge(xn_done, TT * (m + 1))
                for k in chunks:
                    if not first:
                        pe.wait_ge(hid_done, m * FC - 1 + k // 2)
                    for t in range(TT):
                        e = pe.transpose(T_ps[k][:, t * P:(t + 1) * P], xn[:, t, k * P:(k + 1) * P], ident[:])
                    e.then_inc(xt_done, 1)

            def macro_tile(m, last):
                for c in range(FC):
                    if c + 1 < FC:
                        up_gate(m, c + 1)
                    if c == FC - 2 and not last:
                        transposes(m + 1, False, (0, 1))
                    if c == FC - 1 and not last:
                        transposes(m + 1, False, (2, 3))
                    down(m, c)
                if not last:
                    up_gate(m + 1, 0)

            transposes(0, True)
            up_gate(0, 0)
            macro_tile(0, False)
            with pe.Fori(1, NM - 1) as m:
                macro_tile(m, False)
            macro_tile(NM - 1, True)


def quantise(nc, ternary, w_mean, sig_scale, y_scale, y_scale_sq, weights_up, partial, weights):
    COUNT = D * F
    WIDTH = COUNT // P
    with ExitStack() as ctx:
        def sb(name, shape, dt=F32):
            return ctx.enter_context(nc.sbuf_tensor(name, shape, dt))

        FIRST_PART = 3 * WIDTH // 4
        w_gate_here, w_down_here = sb("w_gate_here", [P, WIDTH]), sb("w_down_here", [P, FIRST_PART])
        ones = sb("ones", [P, P])
        total = sb("total", [P, 3])
        half, minus_half_mean = sb("half", [P, 3]), sb("minus_half_mean", [P, 3])
        mean_prod = sb("mean_prod", [P, 2])
        sum_ps = ctx.enter_context(nc.psum_tensor("sum_ps", [P, 3, PARTS], F32))
        names = ("w_gate_in", "w_gate_rest_in", "w_down_in", "w_down_rest_in", "ones_set", "partial_done", "summed",
                 "total_done", "mean_done", "thresholds", "below_done", "ternary_done", "prod_done")
        (w_gate_in, w_gate_rest_in, w_down_in, w_down_rest_in, ones_set, partial_done, summed,
         total_done, mean_done, thresholds, below_done, ternary_done, prod_done) = (
            ctx.enter_context(nc.semaphore(n)) for n in names)
        pieces = (((weights_up[:], 0, WIDTH, None),),
                  ((w_gate_here[:, 0:WIDTH // 2], 0, WIDTH // 2, w_gate_in),
                   (w_gate_here[:, WIDTH // 2:], WIDTH // 2, WIDTH, w_gate_rest_in)),
                  ((w_down_here[:], 0, FIRST_PART, w_down_in),
                   (weights_up[:, 0:WIDTH - FIRST_PART], FIRST_PART, WIDTH, w_down_rest_in)))
        flat = [t[:].rearrange("p c n -> p (c n)") for t in ternary]
        block = ctx.enter_context(nc.Block())

        @block.sync
        def _(sp):
            for n in (1, 2):
                w = weights[n - 1].rearrange("(c p) n -> p c n", p=P)
                cols = weights[n - 1].shape[1]
                for where, begin, end, here in pieces[n]:
                    if here is w_down_in:
                        sp.wait_ge(w_gate_in, 16)
                    if here is w_down_rest_in:
                        sp.wait_ge(ternary_done, 1)
                    sp.dma_start(where.rearrange("p (c n) -> p c n", n=cols),
                                 w[:, begin // cols:end // cols]).then_inc(here, 16)

        @block.scalar
        def _(act):
            part = WIDTH // PARTS
            for n in (1, 2):
                for where, begin, end, here in pieces[n]:
                    act.wait_ge(here, 16)
                    for k in range(begin // part, end // part):
                        e = nc.scalar.activation(flat[n][:, k * part:(k + 1) * part],
                                                 where[:, k * part - begin:(k + 1) * part - begin],
                                                 ACT.Abs, accum_out=partial[:, n, k:k + 1])
                e.then_inc(partial_done, 1)

        @block.tensor
        def _(pe):
            pe.wait_ge(ones_set, 1)
            for n in range(3):
                at_least(pe, partial_done, n)
                at_least(pe, total_done, n)
                pe.matmul(sum_ps[:, n, :], ones[:], partial[:, n, :], start=True, stop=True).then_inc(summed, 1)

        @block.vector
        def _(dve):
            nc.vector.memset(ones[:], 1.0).then_inc(ones_set, 1)
            for n in range(3):
                dve.wait_ge(summed, n + 1)
                nc.vector.tensor_reduce(total[:, n:n + 1], sum_ps[:, n, :], AX.X, ALU.add).then_inc(total_done, 1)
                dve.wait_ge(total_done, n + 1)
                nc.vector.tensor_scalar(w_mean[:, n:n + 1], total[:, n:n + 1], 1.0 / COUNT, 1e-8,
                                        ALU.mult, ALU.add).then_inc(mean_done, 1)
                dve.wait_ge(mean_done, n + 1)
                nc.vector.tensor_scalar(half[:, n:n + 1], w_mean[:, n:n + 1], 0.5, None, ALU.mult).then_inc(thresholds, 1)
                nc.vector.tensor_scalar(minus_half_mean[:, n:n + 1], w_mean[:, n:n + 1], -0.5, None,
                                        ALU.mult).then_inc(thresholds, 1)
                dve.wait_ge(thresholds, 2 * n + 2)
                for where, begin, end, _ in pieces[n]:
                    nc.vector.tensor_scalar(flat[n][:, begin:end], where, minus_half_mean[:, n:n + 1], None,
                                            ALU.is_lt).then_inc(below_done, 1)
                for k, (where, begin, end, _) in enumerate(pieces[n]):
                    dve.wait_ge(below_done, sum(len(p) for p in pieces[:n]) + k + 1)
                    e = nc.vector.scalar_tensor_tensor(flat[n][:, begin:end], where, half[:, n:n + 1],
                                                       flat[n][:, begin:end], ALU.is_gt, ALU.subtract)
                e.then_inc(ternary_done, 1)
            nc.vector.tensor_scalar(sig_scale[:], w_mean[:, 0:1], 1.0 / XN_SCALE, None, ALU.mult).then_inc(prod_done, 1)
            nc.vector.tensor_tensor(mean_prod[:, 0:1], w_mean[:, 0:1], w_mean[:, 1:2], ALU.mult).then_inc(prod_done, 1)
            dve.wait_ge(prod_done, 2)
            nc.vector.tensor_tensor(mean_prod[:, 1:2], mean_prod[:, 0:1], w_mean[:, 2:3], ALU.mult).then_inc(prod_done, 1)
            dve.wait_ge(prod_done, 3)
            nc.vector.tensor_scalar(y_scale[:], mean_prod[:, 1:2], 1.0 / H_SCALE, None, ALU.mult).then_inc(prod_done, 1)
            dve.wait_ge(prod_done, 4)
            nc.vector.tensor_tensor(y_scale_sq[:], y_scale[:], y_scale[:], ALU.mult).then_inc(prod_done, 1)


def rope_tables():
    inv_freq = np.float32(1.0) / np.power(np.float32(10000.0), np.arange(0, HD, 2, dtype=np.float32) / np.float32(HD))
    angle = (np.arange(SEQ, dtype=np.float32)[:, None] * inv_freq[None, :]).astype(np.float64)
    sign = np.where(np.arange(HD) % 2 == 0, -1.0, 1.0)
    cos = np.repeat(np.cos(angle), 2, axis=1)
    sin = np.repeat(np.sin(angle), 2, axis=1) * sign

    def by_tile(t):
        t = np.tile(t.T.astype(np.float32), (P // HD, 1))
        t = t.reshape(P, PER_BATCH, MT).transpose(1, 0, 2)
        return np.ascontiguousarray(np.tile(t, (BATCH, 1, 1)))

    return by_tile(cos), by_tile(sin)


def band_masks():
    q, k = np.arange(P)[:, None], np.arange(2 * P)[None, :]
    seen = (k >= q) & (k <= q + WINDOW)
    masks = np.zeros((NM, P, 2 * P), np.float32)
    for i in range(NM):
        masks[i][~(seen & ((k >= P) | (i % PER_BATCH != 0)))] = NEG
    return masks


def kernel(L0_attn_x, L0_attn_W_qkv, L0_attn_W_out, L0_attn_b_out, L0_ffn_W_up, L0_ffn_W_gate, L0_ffn_W_down):
    import concourse.bacc as bacc
    from concourse.bass_utils import run_bass_kernel_spmd

    cos_t, sin_t = rope_tables()
    arrays = {
        "x": np.ascontiguousarray(L0_attn_x),
        "w_qkv": np.ascontiguousarray(np.asarray(L0_attn_W_qkv).reshape(D, D, 3).transpose(2, 0, 1)),
        "w_out": np.ascontiguousarray(L0_attn_W_out),
        "b_out": np.ascontiguousarray(L0_attn_b_out),
        "w_up": np.ascontiguousarray(np.asarray(L0_ffn_W_up).T),
        "w_gate": np.ascontiguousarray(np.asarray(L0_ffn_W_gate).T),
        "w_down": np.ascontiguousarray(np.asarray(L0_ffn_W_down).T),
        "cos_t": cos_t,
        "sin_t": sin_t,
        "bands": band_masks(),
        "ident": np.eye(P, dtype=np.float32),
    }
    nc = bacc.Bacc("TRN2", target_bir_lowering=False, num_devices=1)
    ins = [nc.dram_tensor(f"in_{k}", a.shape, mybir.dt.from_np(a.dtype), kind="ExternalInput").ap()
           for k, a in arrays.items()]
    out = nc.dram_tensor("out_x", (BATCH, SEQ, D), F32, kind="ExternalOutput").ap()
    layer(nc, *ins, out)
    r = run_bass_kernel_spmd(nc, [{f"in_{k}": a for k, a in arrays.items()}], core_ids=[0])
    return r.results[0]["out_x"]
```
